# Optimizing a Trainium2 kernel written in Bass

```python
import numpy as np
import jax
import jax.numpy as jnp

def _softmax(x, axis=-1):
    return jax.nn.softmax(x, axis=axis)

def _gelu(x):
    return jax.nn.gelu(x, approximate=True)

def _silu(x):
    return jax.nn.silu(x)

def _sigmoid(x):
    return jax.nn.sigmoid(x)

def _layernorm(x, axis=-1, eps=1e-05):
    m = jnp.mean(x, axis=axis, keepdims=True)
    v = jnp.var(x, axis=axis, keepdims=True)
    return (x - m) / jnp.sqrt(v + eps)

def _scatter_add(tgt, idx, src, axis=0):
    return tgt.at[idx].add(src)

def _segment_sum(src, seg, n):
    return jax.ops.segment_sum(src, seg, n)
kernel_name = 'mk_adaln_ffn_d1_seqx_r8_1b29ed'

def setup_inputs(seed: int=0):
    np.random.seed(seed)
    _w = jnp.asarray

    def _rec_inputs():
        import jax
        import jax.numpy as jnp
        _rk = jax.random.key(seed)
        x = 7.22e-05 + 1 * jax.random.normal(jax.random.fold_in(_rk, 1), (128, 32, 128), jnp.float32)
        _lenS = 32 - jax.random.randint(jax.random.fold_in(_rk, 7), (128,), 0, max(1, 32 // 4) + 1, jnp.int32)
        _lenS2 = 32 - jax.random.randint(jax.random.fold_in(_rk, 8), (128,), 0, max(1, 32 // 4) + 1, jnp.int32)
        condB_tauraws = -5.74692 + 0.777674 * jax.random.normal(jax.random.fold_in(_rk, 11), (128,), jnp.float32)
        cond_256 = -0.000235209 + 0.019331 * jax.random.normal(jax.random.fold_in(_rk, 12), (128, 32), jnp.float32)
        condB_bn2 = jnp.zeros((128,), jnp.float32)
        cond_1024 = -4.10585e-05 + 0.0199478 * jax.random.normal(jax.random.fold_in(_rk, 14), (128, 128), jnp.float32)
        return (x, condB_tauraws, cond_256, condB_bn2, cond_1024)
    x, condB_tauraws, cond_256, condB_bn2, cond_1024 = _rec_inputs()

    def _L0_cond_setup():
        import jax, jax.numpy as jnp
        import numpy as np
        import math
        B, T, E, D = (4, 256, 128, 4)

        def _tau_init(t):
            a = 0.1 ** (1.0 / max(t - 1, 1))
            tt = -math.log(max(a, 1e-10))
            return math.log(math.exp(tt) - 1 + 1e-10)

        def causal_ema(b, tau_raw):
            alpha = jnp.exp(-jax.nn.softplus(tau_raw)).astype(b.dtype)

            def step(h, bt):
                h = alpha * h + bt
                return (h, h)
            h0 = jnp.zeros((b.shape[0], b.shape[2]), b.dtype)
            _, hs = jax.lax.scan(step, h0, jnp.swapaxes(b, 0, 1))
            return jnp.swapaxes(hs, 0, 1)
        key = jax.random.key(seed)
        ks = jax.random.split(key, 10)
        s = 0.02
        return {'x': jax.random.normal(ks[0], (B, T, E), jnp.float32), 'tau_ctx': jnp.float32(_tau_init(max(T // 2, 4))), 'tau_raws': jnp.array([_tau_init(max(T // 2 ** i, 2)) for i in range(D)], jnp.float32), 'Wg': jax.random.normal(ks[1], (E, 2 * E), jnp.float32) * s, 'bg': jnp.full((E,), -0.5, jnp.float32), 'Wn1': jax.random.normal(ks[2], (E // 4, E), jnp.float32) * s, 'bn1': jnp.zeros((E // 4,), jnp.float32), 'Wn2': jax.random.normal(ks[3], (D, E // 4), jnp.float32) * s, 'bn2': jnp.zeros((D,), jnp.float32), 'blend': jax.random.normal(ks[4], (D, E), jnp.float32) * s, 'Wsoma': jax.random.normal(ks[5], (E, E), jnp.float32) * s, 'bsoma': jnp.zeros((E,), jnp.float32), 'Wtemp': jax.random.normal(ks[6], (E, E), jnp.float32) * s, 'btemp': jnp.zeros((E,), jnp.float32), 'Wout': jax.random.normal(ks[7], (E, E), jnp.float32) * s, 'gamma': jnp.ones((E,), jnp.float32), 'beta': jnp.zeros((E,), jnp.float32)}
    _L0_cond_all = _L0_cond_setup()
    _L0_cond_in = {k: v for k, v in _L0_cond_all.items() if k in ('tau_ctx', 'Wg', 'bg', 'Wn1', 'bn1', 'Wsoma', 'bsoma', 'Wtemp', 'btemp', 'Wout', 'gamma', 'beta')}
    del _L0_cond_all

    def _L0_ffn_setup():
        import jax, jax.numpy as jnp
        import numpy as np
        CAPACITY_FACTOR = 0.5
        key = jax.random.key(seed)
        ks = jax.random.split(key, 5)
        B, S, D, F = (4, 512, 128, 512)
        scale_in = 1.0 / np.sqrt(D)
        scale_ff = 1.0 / np.sqrt(F)
        return {'hidden_states': jax.random.normal(ks[0], (B, S, D), dtype=jnp.float32), 'w_router': jax.random.normal(ks[1], (D,), dtype=jnp.float32) * scale_in, 'W1': jax.random.normal(ks[2], (D, F), dtype=jnp.float32) * scale_in, 'b1': jnp.zeros((F,), dtype=jnp.float32), 'W2': jax.random.normal(ks[3], (F, D), dtype=jnp.float32) * scale_ff, 'b2': jnp.zeros((D,), dtype=jnp.float32)}
    _L0_ffn_all = _L0_ffn_setup()
    _L0_ffn_in = {k: v for k, v in _L0_ffn_all.items() if k in ('w_router', 'W1', 'b1', 'W2', 'b2')}
    del _L0_ffn_all
    return {'x': x, 'condB_tauraws': condB_tauraws, 'cond_256': cond_256, 'condB_bn2': condB_bn2, 'cond_1024': cond_1024, 'L0_cond_tau_ctx': _L0_cond_in['tau_ctx'], 'L0_cond_Wg': _L0_cond_in['Wg'], 'L0_cond_bg': _L0_cond_in['bg'], 'L0_cond_Wn1': _L0_cond_in['Wn1'], 'L0_cond_bn1': _L0_cond_in['bn1'], 'L0_cond_Wsoma': _L0_cond_in['Wsoma'], 'L0_cond_bsoma': _L0_cond_in['bsoma'], 'L0_cond_Wtemp': _L0_cond_in['Wtemp'], 'L0_cond_btemp': _L0_cond_in['btemp'], 'L0_cond_Wout': _L0_cond_in['Wout'], 'L0_cond_gamma': _L0_cond_in['gamma'], 'L0_cond_beta': _L0_cond_in['beta'], 'L0_ffn_w_router': _L0_ffn_in['w_router'], 'L0_ffn_W1': _L0_ffn_in['W1'], 'L0_ffn_b1': _L0_ffn_in['b1'], 'L0_ffn_W2': _L0_ffn_in['W2'], 'L0_ffn_b2': _L0_ffn_in['b2']}

def reference(x, condB_tauraws, cond_256, condB_bn2, cond_1024, L0_cond_tau_ctx, L0_cond_Wg, L0_cond_bg, L0_cond_Wn1, L0_cond_bn1, L0_cond_Wsoma, L0_cond_bsoma, L0_cond_Wtemp, L0_cond_btemp, L0_cond_Wout, L0_cond_gamma, L0_cond_beta, L0_ffn_w_router, L0_ffn_W1, L0_ffn_b1, L0_ffn_W2, L0_ffn_b2):
    import jax
    import jax.numpy as jnp

    def _L0_cond_ref(x, tau_ctx, tau_raws, Wg, bg, Wn1, bn1, Wn2, bn2, blend, Wsoma, bsoma, Wtemp, btemp, Wout, gamma, beta):
        import jax, jax.numpy as jnp
        import numpy as np
        import math
        B, T, E, D = (4, 256, 128, 4)

        def _tau_init(t):
            a = 0.1 ** (1.0 / max(t - 1, 1))
            tt = -math.log(max(a, 1e-10))
            return math.log(math.exp(tt) - 1 + 1e-10)

        def causal_ema(b, tau_raw):
            alpha = jnp.exp(-jax.nn.softplus(tau_raw)).astype(b.dtype)

            def step(h, bt):
                h = alpha * h + bt
                return (h, h)
            h0 = jnp.zeros((b.shape[0], b.shape[2]), b.dtype)
            _, hs = jax.lax.scan(step, h0, jnp.swapaxes(b, 0, 1))
            return jnp.swapaxes(hs, 0, 1)
        ctx = causal_ema(x, tau_ctx)
        gate_in = jnp.concatenate([x, ctx], axis=-1)
        wg = jax.nn.sigmoid(jnp.einsum('btc,ec->bte', gate_in, Wg) + bg)
        gated = x * wg
        h1 = jax.nn.gelu(jnp.einsum('btc,hc->bth', x, Wn1) + bn1, approximate=False)
        mod = 0.5 + jax.nn.sigmoid(jnp.einsum('bth,dh->btd', h1, Wn2) + bn2)
        traces = jax.vmap(lambda tau, m: causal_ema(gated * m[..., None], tau))(tau_raws, jnp.moveaxis(mod, -1, 0))
        blend_w = jax.nn.softmax(blend, axis=0)
        temporal = jnp.einsum('dbtc,dc->btc', traces, blend_w)
        gate = jax.nn.sigmoid(jnp.einsum('btc,ec->bte', temporal, Wtemp) + btemp)
        soma = jax.nn.gelu(jnp.einsum('btc,ec->bte', x, Wsoma) + bsoma, approximate=False)
        out = jnp.einsum('btc,ec->bte', soma * gate, Wout)
        mu = out.mean(-1, keepdims=True)
        var = out.var(-1, keepdims=True)
        return (out - mu) / jnp.sqrt(var + 1e-05) * gamma + beta

    def _L0_ffn_ref(hidden_states, w_router, W1, b1, W2, b2):
        import jax, jax.numpy as jnp
        import numpy as np
        CAPACITY_FACTOR = 0.5
        'Mixture-of-Depths block: route top-k tokens through an FFN inner block,\n            scatter back with sigmoid router weights; bypassed tokens pass through.'
        B, S, D = hidden_states.shape
        k = int(S * CAPACITY_FACTOR)
        scores = jnp.einsum('bsd,d->bs', hidden_states, w_router)
        top_scores, top_idx = jax.lax.top_k(scores, k)
        weights = jax.nn.sigmoid(top_scores)
        selected = jnp.take_along_axis(hidden_states, top_idx[:, :, None], axis=1)
        h = jax.nn.gelu(jnp.einsum('bkd,df->bkf', selected, W1) + b1)
        processed = jnp.einsum('bkf,fd->bkd', h, W2) + b2
        update = weights[:, :, None] * processed

        def scatter_one(xb, ib, ub):
            return xb.at[ib].add(ub)
        output = jax.vmap(scatter_one)(hidden_states, top_idx, update)
        return output
    x = x + _L0_ffn_ref(_L0_cond_ref(x, L0_cond_tau_ctx, condB_tauraws, L0_cond_Wg, L0_cond_bg, L0_cond_Wn1, L0_cond_bn1, cond_256, condB_bn2, cond_1024, L0_cond_Wsoma, L0_cond_bsoma, L0_cond_Wtemp, L0_cond_btemp, L0_cond_Wout, L0_cond_gamma, L0_cond_beta), L0_ffn_w_router, L0_ffn_W1, L0_ffn_b1, L0_ffn_W2, L0_ffn_b2)
    return x

_drawn_inputs = setup_inputs


def setup_inputs(seed=0):
    import zlib

    import numpy as np

    out = dict(_drawn_inputs(seed))
    spreads = {'condB_bn2': (0.0, 2.0),
     'L0_cond_bg': (-0.5, 0.6),
     'L0_cond_bn1': (0.0, 2.0),
     'L0_cond_bsoma': (0.0, 0.1),
     'L0_cond_btemp': (0.0, 0.1),
     'L0_cond_gamma': (1.0, 0.2),
     'L0_cond_beta': (0.0, 0.1),
     'L0_ffn_b1': (0.0, 0.398),
     'L0_ffn_b2': (0.0, 0.1)}
    factors = {'condB_tauraws': 8.0, 'cond_256': 200.0, 'cond_1024': 200.0, 'L0_cond_Wn1': 200.0}
    for name, (base, spread) in spreads.items():
        noise = np.random.default_rng([zlib.crc32(name.encode()), seed]).standard_normal(out[name].shape)
        drawn = base * np.exp(spread * noise) if base else spread * noise
        out[name] = jnp.asarray(drawn.astype(out[name].dtype))
    for name, factor in factors.items():
        out[name] = (out[name] * factor).astype(out[name].dtype)
    return out
```

```python
from contextlib import ExitStack

import concourse.bass as bass
from concourse import mybir

P = 128
B, T, E, D, F, HN = 128, 32, 128, 128, 512, 32
TOPK = T // 2
L = T // 2
G = 2
BG = B // G
COLS = BG * T
BT = P // T
NT = COLS // P
QT = 4
NQ = NT // QT
BQ = BT * QT
SEL = BT * TOPK
NS = NT * SEL // P
NF = F // P
BANK = 512
SLOT = 2 * BANK
OW = E + 2

ALU = mybir.AluOpType
ACT = mybir.ActivationFunctionType
AX_X = mybir.AxisListType.X
F32 = mybir.dt.float32
BF16 = mybir.dt.bfloat16

UNITS = [(lag, (c,)) for lag in range(L // 2) for c in range(2)] + [(lag, (0, 1)) for lag in range(L // 2, L)]


def stage_a(g):
    two = range(2)
    return ([("xt", g, i) for i in two] + [("soma", g, i) for i in two] + [("h1", g, i) for i in two]
            + [("wg", g, i) for i in two] + [("mod", g, i) for i in two])


def stage_b(g):
    out, per = [], len(UNITS) // NQ
    for q in range(NQ):
        k = [("unit", g, per * q + i) for i in range(per)]
        out += [("nat", g, q)] + k[:2] + [("state", g, q)] + k[2:4] + [("carry", g, q)] + k[4:]
    return out


def stage_c(g):
    return ([("gate", g, i) for i in range(2)] + [("out", g, q) for q in range(NQ)]
            + [("norm", g, 0), ("pick", g, 0), ("gather", g, 0), ("turn", g, 0)]
            + [("up", g, f) for f in range(NF)] + [("down", g, 0)] + [("scatter", g, i) for i in range(2)])


def merged(a, b):
    out, n = [], 0
    for i, step in enumerate(a):
        out.append(step)
        while n < len(b) and (n + 1) * len(a) <= (i + 1) * len(b):
            out.append(b[n])
            n += 1
    return out + b[n:]


STEPS = stage_a(0) + stage_a(1) + stage_b(0) + merged(stage_b(1), stage_c(0)) + stage_c(1)
READERS = {"xt": 1, "soma": 1, "h1": 1, "wg": 1, "mod": 1, "nat": 2, "carry": 1, "unit": 1, "gate": 1,
           "out": 1, "gather": 1, "turn": 1, "up": 1, "down": 1, "scatter": 1}
RING = [s for s in STEPS if s[0] in READERS]
USE = {s: n for n, s in enumerate(RING)}
NSLOT = 2


def filled(step):
    return USE[step] // NSLOT + 1


def reads_before(step):
    n = USE[step]
    return sum(READERS[s[0]] for s in RING[n % NSLOT:n:NSLOT])


def reads_after(step):
    return reads_before(step) + READERS[step[0]]


def adaln_ffn(nc, x, tau_raws, w_n2, b_n2, blend, tau_ctx, w_g, b_g, w_n1, b_n1, w_soma, b_soma,
              w_temp, b_temp, w_out, gamma, beta, w_router, w_1, b_1, w_2, b_2, out):
    with ExitStack() as ctx:
        def sb(name, shape, dt=F32):
            return ctx.enter_context(nc.sbuf_tensor(name, shape, dt))

        def sem(name):
            return ctx.enter_context(nc.semaphore(name))

        slots = [ctx.enter_context(nc.psum_tensor(f"slot{i}", [P, SLOT], F32)) for i in range(NSLOT)]
        st_ps = ctx.enter_context(nc.psum_tensor("st_ps", [P, BT, BANK], F32))

        ident = sb("ident", [P, P])
        ones = sb("ones", [P, P])
        wg_in = sb("wg_in", [P, 2 * E])
        wn1_in = sb("wn1_in", [HN, E])
        wn2_in = sb("wn2_in", [P, HN])
        blend_in = sb("blend_in", [P, E])
        wsoma_in = sb("wsoma_in", [P, E])
        wtemp_in = sb("wtemp_in", [P, E])
        wout_in = sb("wout_in", [P, E])
        w1_sb = sb("w1_sb", [P, F])
        w2_sb = sb("w2_sb", [P, NF, E])
        turned1 = sb("turned1", [P, 3 * P + HN])
        wgx_t, wgc_t, wsoma_t = (turned1[:, i * P:(i + 1) * P] for i in range(3))
        wn1_t = turned1[:, 3 * P:3 * P + HN]
        wn2_t = sb("wn2_t", [HN, D])
        wtemp_t = sb("wtemp_t", [P, E])
        wout_t = sb("wout_t", [P, E + 2])
        bg, bsoma, btemp = sb("bg", [P, 1]), sb("bsoma", [P, 1]), sb("btemp", [P, 1])
        bn1, bn2 = sb("bn1", [HN, 1]), sb("bn2", [P, 1])
        gamma_c, beta_c, router = sb("gamma_c", [P, 1]), sb("beta_c", [P, 1]), sb("router", [P, 1])
        b1_c = sb("b1_c", [P, NF])
        gamma_r, beta_r, b2_r = sb("gamma_r", [P, E]), sb("beta_r", [P, E]), sb("b2_r", [P, E])
        taus = sb("taus", [P, 2])
        tau_e = sb("tau_e", [P, 2])
        tau_s = sb("tau_s", [P, 2])
        alphas = sb("alphas", [P, 2])
        alpha, alpha_ctx = alphas[:, 0:1], alphas[:, 1:2]
        smax, ssum, srec = sb("smax", [P, 1]), sb("ssum", [P, 1]), sb("srec", [P, 1])
        sexp = sb("sexp", [P, P])
        blend_t = sb("blend_t", [P, P])
        decayed = sb("decayed", [P, L, E])
        powers = sb("powers", [P, L + 1])
        tail_row = sb("tail_row", [P, BT, T])
        tail = sb("tail", [P, D])
        rw = sb("rw", [P, 2])
        rsum = sb("rsum", [P, 2])
        rank_of = sb("rank_of", [P, SEL])
        before = sb("before", [P, T, T], BF16)

        x_nat = sb("x_nat", [P, G, NT, E])
        x_t = sb("x_t", [P, G, COLS])
        ctx_acc = sb("ctx_acc", [P, G, COLS])
        gm = sb("gm", [P, G, 2, COLS])
        soma = sb("soma", [P, G, COLS])
        h1 = sb("h1", [HN, COLS])
        mod_nat = sb("mod_nat", [P, 2, QT, D])
        gated_nat = sb("gated_nat", [P, 2, QT, E])
        state = sb("state", [P, BT, QT, E])
        carried = sb("carried", [P, BG, L])
        NP = 2
        prod = sb("prod", [P, NP, SLOT])
        prod_res = sb("prod_res", [P, NT // 2, E])
        o_sb = sb("o_sb", [P, NT, OW])
        stats = sb("stats", [P, NT, 6])
        small = sb("small", [P, 10, NT])
        score = sb("score", [P, T])
        score_b = sb("score_b", [P, T])
        gt = sb("gt", [P, T, T], BF16)
        eq = sb("eq", [P, T, T], BF16)
        rank_b = sb("rank_b", [P, T])
        rank_n = sb("rank_n", [P, T])
        weight = sb("weight", [P, NT])
        pick = sb("pick", [P, NT, SEL])
        pick_t = sb("pick_t", [P, NS, P])
        hid_t = sb("hid_t", [P, NT * SEL])
        down = sb("down", [P, NS, E])

        x_in = [sem(f"x_in{i}") for i in range(G * 2)]
        w_in, rest_in = sem("w_in"), sem("rest_in")
        own_pool, own_dve = sem("own_pool"), sem("own_dve")
        consts = sem("consts")
        turned = sem("turned")
        tabled = sem("tabled")
        exped = sem("exped")
        slot_full = [sem(f"slot_full{i}") for i in range(NSLOT)]
        slot_read = [sem(f"slot_read{i}") for i in range(NSLOT)]
        ctx_done = sem("ctx_done")
        gated_done, mod_done = sem("gated_done"), sem("mod_done")
        state_full, state_read = sem("state_full"), sem("state_read")
        acc_done = sem("acc_done")
        sg_done = sem("sg_done")
        var_done, std_done = sem("var_done"), sem("std_done")
        norm_done = sem("norm_done")
        score_done, sig_done = sem("score_done"), sem("sig_done")
        pick_done = sem("pick_done")
        res_done, xb_done = sem("res_done"), sem("xb_done")
        y_out = sem("y_out")

        x_dram = x.rearrange("b t e -> (b t) e").rearrange("(h n p) e -> h p n e", p=P, n=NT // 2)
        y_dram = out.rearrange("b t e -> (b t) e").rearrange("(h n p) e -> h p n e", p=P, n=NT // 2)

        def col(v):
            return v.rearrange("(p o) -> p o", o=1)

        def row(v):
            return v.rearrange("(o n) -> o n", o=1).to_broadcast([P, v.shape[0]])

        def halves(buf, h):
            return buf[:, h // 2, (h % 2) * (NT // 2):(h % 2 + 1) * (NT // 2), :]

        def slot(step):
            return slots[USE[step] % NSLOT]

        def full(step):
            return slot_full[USE[step] % NSLOT]

        def read(step):
            return slot_read[USE[step] % NSLOT]

        def tile_cols(buf, g, n):
            return buf[:, g, n * P:(n + 1) * P]

        gated = gm[:, :, 0, :]
        mod = gm[:, :, 1, :]
        inner = gm[:, :, :, :].rearrange("p g m n -> p g (m n)")

        def lagged(buf, k, shift=0):
            lag, chunks = UNITS[k]
            per = T // len(chunks)
            t0 = (chunks[0] * L if len(chunks) == 1 else 0) + shift * lag
            return buf.rearrange("p (h b t) -> p h b t", h=2, t=per)[:, :, :, t0:t0 + L - lag]

        def in_slot(buf, k):
            lag, chunks = UNITS[k]
            n = BG // 2 * len(chunks) * (L - lag)
            return buf.rearrange("p (h n) -> p h n", h=2)[:, :, 0:n].rearrange("p h (b t) -> p h b t", t=L - lag)

        ADDED = {s: n for n, s in enumerate(s for s in STEPS if s[0] == "unit" and UNITS[s[2]][0] > 0)}
        PER_G = len(ADDED) // G

        def sums_to(n):
            return n // PER_G * (PER_G + 1) + n % PER_G + 1

        block = ctx.enter_context(nc.Block())

        @block.sync
        def _(sp):
            for h in range(G * 2):
                sp.dma_start(halves(x_nat, h), x_dram[h]).then_inc(x_in[h], 16)
            sp.dma_start(w1_sb[:, :], w_1).then_inc(rest_in, 16)
            sp.dma_start(w2_sb[:, :, :], w_2.rearrange("(k p) e -> p k e", p=P)).then_inc(rest_in, 16)
            sp.dma_start(b1_c[:, :], b_1.rearrange("(k p) -> p k", p=P),
                         allow_slow_non_contiguous=True).then_inc(rest_in, 16)
            sp.dma_start(gamma_r[:, :], row(gamma)).then_inc(rest_in, 16)
            sp.dma_start(beta_r[:, :], row(beta)).then_inc(rest_in, 16)
            sp.dma_start(b2_r[:, :], row(b_2)).then_inc(rest_in, 16)
            for h in range(G * 2):
                step = ("scatter", h // 2, h % 2)
                sp.wait_ge(read(step), reads_after(step))
                sp.dma_start(y_dram[h], halves(x_nat, h)).then_inc(y_out, 16)
            sp.wait_ge(y_out, G * 2 * 16)

        REST = 6 * 16
        W_ALL = 17 * 16

        @block.gpsimd
        def _(pool):
            nc.gpsimd.memset(ident[:, :], 0.0).then_inc(own_pool, 1)
            nc.gpsimd.memset(ones[:, :], 1.0).then_inc(own_pool, 1)
            nc.gpsimd.memset(before[:, :, :], 1.0).then_inc(own_pool, 1)
            nc.gpsimd.iota(rank_of[:, :], pattern=[[0, BT], [1, TOPK]], base=0, channel_multiplier=0,
                           allow_small_or_imprecise_dtypes=True).then_inc(own_pool, 1)
            pool.wait_ge(own_pool, 4)
            nc.gpsimd.affine_select(out=ident[:, :], in_=ident[:, :], compare_op=ALU.not_equal, fill=1.0,
                                    base=0, pattern=[[-1, P]], channel_multiplier=1).then_inc(consts, 1)
            places = rank_of[:, :].rearrange("p (b j) -> p b j", b=BT)
            nc.gpsimd.affine_select(out=places, in_=places, compare_op=ALU.is_ge, fill=-1.0, base=0,
                                    pattern=[[-T, BT], [0, TOPK]], channel_multiplier=1).then_inc(own_pool, 1)
            pool.wait_ge(own_pool, 5)
            nc.gpsimd.affine_select(out=places, in_=places, compare_op=ALU.is_ge, fill=-1.0, base=T - 1,
                                    pattern=[[T, BT], [0, TOPK]], channel_multiplier=-1).then_inc(consts, 1)
            nc.gpsimd.affine_select(out=before[:, :, :], in_=before[:, :, :], compare_op=ALU.is_ge, fill=0.0,
                                    base=-1, pattern=[[1, T], [-1, T]], channel_multiplier=0).then_inc(consts, 1)
            pool.wait_ge(rest_in, REST)
            own = 5
            for step in STEPS:
                kind, g, k = step
                if kind == "xt":
                    pool.wait_ge(read(step), reads_after(step))
                    h = halves(x_nat, 2 * g + k)
                    nc.gpsimd.tensor_tensor(h, h, beta_r[:, None, :].to_broadcast([P, NT // 2, E]),
                                            ALU.add).then_inc(xb_done, 1)
                if step in ADDED:
                    n = ADDED[step]
                    dst = lagged(ctx_acc[:, g, :], k, shift=1)
                    pool.wait_ge(read(step), reads_after(step))
                    if n % PER_G:
                        pool.wait_ge(acc_done, sums_to(n) - 1)
                    nc.gpsimd.tensor_tensor(dst, dst, in_slot(prod[:, n % NP, :], k),
                                            ALU.add).then_inc(acc_done, 1)
                if kind == "unit" and k == len(UNITS) - 1:
                    for q in range(NQ):
                        pool.wait_ge(read(("carry", g, q)), reads_after(("carry", g, q)))
                    pool.wait_ge(acc_done, (g + 1) * (PER_G + 1) - 1)
                    dst = ctx_acc[:, g, :].rearrange("p (b t) -> p b t", t=T)[:, :, L:]
                    nc.gpsimd.tensor_tensor(dst, dst, carried[:, :, :], ALU.add).then_inc(acc_done, 1)
                if kind == "norm":
                    for i in range(2):
                        r = halves(x_nat, 2 * g + i)
                        pool.wait_ge(norm_done, g * NT + (i + 1) * NT // 2)
                        if 2 * g + i:
                            pool.wait_ge(res_done, 2 * g + i)
                        nc.gpsimd.tensor_tensor(
                            prod_res[:, :, :], o_sb[:, i * NT // 2:(i + 1) * NT // 2, 0:E],
                            gamma_r[:, None, :].to_broadcast([P, NT // 2, E]), ALU.mult).then_inc(own_pool, 1)
                        own += 1
                        pool.wait_ge(own_pool, own)
                        pool.wait_ge(xb_done, 2 * g + i + 1)
                        nc.gpsimd.tensor_tensor(r, r, prod_res[:, :, :], ALU.add).then_inc(res_done, 1)

        @block.scalar
        def _(act):
            for dst, src in (
                (wsoma_in[:, :], w_soma), (wn1_in[:, :], w_n1), (wg_in[:, :], w_g), (wn2_in[:, :], w_n2),
                (blend_in[:, :], blend), (wtemp_in[:, :], w_temp), (wout_in[:, :], w_out),
                (taus[:, 0:1], col(tau_raws)), (taus[:, 1:2], tau_ctx.to_broadcast([P, 1])),
                (bsoma[:, :], col(b_soma)), (bn1[:, :], col(b_n1)), (bg[:, :], col(b_g)), (bn2[:, :], col(b_n2)),
                (btemp[:, :], col(b_temp)), (gamma_c[:, :], col(gamma)), (beta_c[:, :], col(beta)),
                (router[:, :], col(w_router)),
            ):
                act.dma_start(dst, src).then_inc(w_in, 16)
            act.wait_ge(w_in, W_ALL)
            nc.scalar.activation(tau_e[:, :], taus[:, :], ACT.Exp).then_inc(exped, 1)
            act.wait_ge(tabled, 1)
            nc.scalar.activation(sexp[:, :], blend_t[:, :], ACT.Exp, bias=smax[:, :],
                                 accum_out=ssum[:, :]).then_inc(exped, 1)
            for step in STEPS:
                kind, g, k = step
                half = slice(k * SLOT, (k + 1) * SLOT)
                if kind in ("xt", "soma", "h1", "wg", "mod", "nat", "carry", "gate", "out", "gather", "turn", "up"):
                    act.wait_ge(full(step), filled(step))
                if kind == "xt":
                    nc.scalar.activation(x_t[:, g, half], slot(step)[:, :], ACT.Copy).then_inc(read(step), 1)
                elif kind == "soma":
                    nc.scalar.activation(soma[:, g, half], slot(step)[:, :], ACT.Gelu,
                                         bias=bsoma[:, :]).then_inc(read(step), 1)
                elif kind == "h1":
                    if g:
                        last = ("mod", g - 1, k)
                        act.wait_ge(full(last), filled(last))
                    nc.scalar.activation(h1[:, half], slot(step)[0:HN, :], ACT.Gelu,
                                         bias=bn1[:, :]).then_inc(read(step), 1)
                elif kind == "wg":
                    nc.scalar.activation(gated[:, g, half], slot(step)[:, :], ACT.Sigmoid,
                                         bias=bg[:, :]).then_inc(read(step), 1)
                elif kind == "mod":
                    nc.scalar.activation(mod[:, g, half], slot(step)[:, :], ACT.Sigmoid,
                                         bias=bn2[:, :]).then_inc(read(step), 1)
                elif kind == "nat":
                    q = g * NQ + k
                    if q >= 2:
                        act.wait_ge(state_full, q - 1)
                    nc.scalar.activation(gated_nat[:, q % 2, :, :].rearrange("p n e -> p (n e)"),
                                         slot(step)[:, BANK:], ACT.Copy).then_inc(read(step), 1)
                elif kind == "carry":
                    if g and k == 0:
                        act.wait_ge(acc_done, g * (PER_G + 1))
                    dst = carried[:, k * BQ:(k + 1) * BQ, :].rearrange("p b t -> p (b t)")
                    nc.scalar.activation(dst, slot(step)[:, 0:BQ * L], ACT.Copy).then_inc(read(step), 1)
                elif kind == "gate":
                    nc.scalar.activation(x_t[:, g, half], slot(step)[:, :], ACT.Sigmoid,
                                         bias=btemp[:, :]).then_inc(read(step), 1)
                elif kind == "out":
                    if g and k == 0:
                        last = ("gather", g - 1, 0)
                        act.wait_ge(res_done, 2 * g)
                        act.wait_ge(full(last), filled(last))
                    src = slot(step)[:, :].rearrange("p (h n) -> p h n", h=2)[:, :, 0:2 * OW]
                    dst = o_sb[:, k * QT:(k + 1) * QT, :].rearrange("p (h n) w -> p h (n w)", h=2)
                    nc.scalar.activation(dst, src, ACT.Copy).then_inc(read(step), 1)
                elif kind == "norm":
                    act.wait_ge(var_done, g + 1)
                    nc.scalar.activation(small[:, 6, :], small[:, 5, :], ACT.Sqrt).then_inc(std_done, 1)
                elif kind == "pick":
                    act.wait_ge(score_done, g + 1)
                    nc.scalar.activation(small[:, 9, :], score[:, 0:NT], ACT.Sigmoid).then_inc(sig_done, 1)
                elif kind == "gather":
                    nc.scalar.activation(hid_t[:, :], slot(step)[:, :], ACT.Identity, bias=beta_c[:, :],
                                         scale=gamma_c[:, :]).then_inc(read(step), 1)
                elif kind == "turn":
                    nc.scalar.activation(pick_t[:, :, :].rearrange("p n k -> p (n k)"), slot(step)[:, :],
                                         ACT.Copy).then_inc(read(step), 1)
                elif kind == "up":
                    nc.scalar.activation(inner[:, g, k * SLOT:(k + 1) * SLOT], slot(step)[:, :],
                                         ACT.Gelu_apprx_tanh, bias=b1_c[:, k:k + 1]).then_inc(read(step), 1)

        @block.vector
        def _(dve):
            own = [0]

            def settled():
                own[0] += 1
                return own[0]

            nc.vector.memset(powers[:, 0:1], 1.0).then_inc(own_dve, 1)
            dve.wait_ge(own_dve, settled())
            nc.vector.memset(score[:, :], 0.0).then_inc(own_dve, 1)
            dve.wait_ge(own_dve, settled())
            nc.vector.memset(tail_row[:, :, :], 1.0).then_inc(own_dve, 1)
            dve.wait_ge(own_dve, settled())
            dve.wait_ge(turned, 2)
            nc.vector.tensor_copy(blend_t[:, :], st_ps[:, 1, 3 * P:4 * P]).then_inc(own_dve, 1)
            dve.wait_ge(own_dve, settled())
            nc.vector.tensor_reduce(smax[:, :], blend_t[:, :], AX_X, ALU.max, negate=True).then_inc(tabled, 1)
            nc.vector.tensor_copy(turned1[:, :], st_ps[:, 0, 0:3 * P + HN]).then_inc(own_dve, 1)
            dve.wait_ge(own_dve, settled())
            nc.vector.tensor_copy(wn2_t[:, :], st_ps[0:HN, 1, 0:P]).then_inc(own_dve, 1)
            dve.wait_ge(own_dve, settled())
            nc.vector.tensor_copy(wtemp_t[:, :], st_ps[:, 1, P:2 * P]).then_inc(own_dve, 1)
            dve.wait_ge(own_dve, settled())
            nc.vector.tensor_copy(wout_t[:, 0:E], st_ps[:, 1, 2 * P:3 * P]).then_inc(tabled, 1)
            dve.wait_ge(w_in, W_ALL)
            nc.vector.tensor_tensor(rw[:, 0:1], gamma_c[:, :], router[:, :], ALU.mult).then_inc(own_dve, 1)
            dve.wait_ge(own_dve, settled())
            nc.vector.tensor_tensor(rw[:, 1:2], beta_c[:, :], router[:, :], ALU.mult).then_inc(tabled, 1)
            dve.wait_ge(exped, 1)
            nc.vector.tensor_scalar(tau_s[:, :], tau_e[:, :], 1.0, None, ALU.add).then_inc(own_dve, 1)
            dve.wait_ge(own_dve, settled())
            nc.vector.reciprocal(alphas[:, :], tau_s[:, :]).then_inc(own_dve, 1)
            dve.wait_ge(own_dve, settled())
            dve.wait_ge(consts, 3)
            nc.vector.tensor_tensor_scan(powers[:, 1:L + 1], alpha.to_broadcast([P, L]), ones[:, 0:L], 1.0,
                                         ALU.mult, ALU.mult).then_inc(own_dve, 1)
            dve.wait_ge(own_dve, settled())
            dve.wait_ge(exped, 2)
            nc.vector.reciprocal(srec[:, :], ssum[:, :]).then_inc(own_dve, 1)
            dve.wait_ge(own_dve, settled())
            nc.vector.tensor_scalar(sexp[:, :], sexp[:, :], srec[:, :], None, ALU.mult).then_inc(own_dve, 1)
            dve.wait_ge(own_dve, settled())
            for t in range(L):
                last = nc.vector.tensor_copy(tail_row[:, :, t:t + 1],
                                             powers[:, None, L - 1 - t:L - t].to_broadcast([P, BT, 1]))
            last.then_inc(tabled, 1)
            dve.wait_ge(turned, 3)
            nc.vector.tensor_copy(decayed[:, 0, :], st_ps[:, 2, 0:P]).then_inc(own_dve, 1)
            dve.wait_ge(own_dve, settled())
            for lag in range(1, L):
                nc.vector.tensor_scalar(decayed[:, lag, :], decayed[:, lag - 1, :], alpha, None,
                                        ALU.mult).then_inc(own_dve, 1)
                dve.wait_ge(own_dve, settled())
            nc.vector.tensor_copy(tail[:, :], st_ps[:, 2, P:2 * P]).then_inc(own_dve, 1)
            dve.wait_ge(own_dve, settled())
            dve.wait_ge(turned, 4)
            nc.vector.tensor_copy(wout_t[:, E:E + 2], st_ps[:, 3, 0:2]).then_inc(own_dve, 1)
            dve.wait_ge(own_dve, settled())
            nc.vector.tensor_copy(rsum[:, :], st_ps[:, 3, 2:4]).then_inc(tabled, 1)

            for step in STEPS:
                kind, g, k = step
                half = slice(k * SLOT, (k + 1) * SLOT)
                if kind == "xt" and k == 1:
                    for i in range(2):
                        dve.wait_ge(read(("xt", g, i)), reads_after(("xt", g, i)))
                    sums = ctx_acc[:, g, :].rearrange("p (b t) -> p t b", t=T)
                    xs = x_t[:, g, :].rearrange("p (b t) -> p t b", t=T)
                    nc.vector.tensor_copy(sums[:, 0, :], xs[:, 0, :]).then_inc(own_dve, 1)
                    dve.wait_ge(own_dve, settled())
                    for t in range(1, T):
                        last = nc.vector.scalar_tensor_tensor(
                            out=sums[:, t, :], in0=sums[:, t - 1, :], scalar=alpha_ctx, in1=xs[:, t, :],
                            op0=ALU.mult, op1=ALU.add)
                        if t < T - 1:
                            last.then_inc(own_dve, 1)
                            dve.wait_ge(own_dve, settled())
                    last.then_inc(ctx_done, 1)
                elif kind == "wg":
                    dve.wait_ge(read(step), reads_after(step))
                    nc.vector.tensor_tensor(gated[:, g, half], gated[:, g, half], x_t[:, g, half],
                                            ALU.mult).then_inc(gated_done, 1)
                elif kind == "mod":
                    dve.wait_ge(read(step), reads_after(step))
                    nc.vector.tensor_scalar(mod[:, g, half], mod[:, g, half], 0.5, None,
                                            ALU.add).then_inc(mod_done, 1)
                elif kind == "nat":
                    q = g * NQ + k
                    dve.wait_ge(full(step), filled(step))
                    if q >= 2:
                        dve.wait_ge(state_full, q - 1)
                    nc.vector.tensor_tensor(
                        mod_nat[:, q % 2, :, :], slot(step)[:, 0:BANK].rearrange("p (n d) -> p n d", n=QT),
                        tail[:, None, :].to_broadcast([P, QT, D]), ALU.mult).then_inc(read(step), 1)
                elif kind == "state":
                    q = g * NQ + k
                    dve.wait_ge(state_full, q + 1)
                    if q:
                        last = ("carry", (q - 1) // NQ, (q - 1) % NQ)
                        dve.wait_ge(full(last), filled(last))
                    nc.vector.tensor_tensor(
                        state[:, :, :, :].rearrange("p b n e -> p (b n) e"),
                        st_ps[:, :, :].rearrange("p b (n e) -> p (b n) e", e=E),
                        decayed[:, 0:1, :].to_broadcast([P, BQ, E]), ALU.mult).then_inc(state_read, 1)
                elif kind == "unit":
                    dve.wait_ge(full(step), filled(step))
                    dve.wait_ge(gated_done, 2 * (g + 1))
                    src = in_slot(slot(step)[:, :], k)
                    if step in ADDED:
                        n = ADDED[step]
                        if n >= NP:
                            dve.wait_ge(acc_done, sums_to(n - NP))
                        dst = in_slot(prod[:, n % NP, :], k)
                    else:
                        dst = lagged(ctx_acc[:, g, :], k, shift=1)
                    nc.vector.tensor_tensor(dst, src, lagged(gated[:, g, :], k),
                                            ALU.mult).then_inc(read(step), 1)
                elif kind == "gate":
                    dve.wait_ge(read(step), reads_after(step))
                    nc.vector.tensor_tensor(x_t[:, g, half], x_t[:, g, half], soma[:, g, half],
                                            ALU.mult).then_inc(sg_done, 1)
                elif kind == "out":
                    dve.wait_ge(read(step), reads_after(step))
                    for n in range(k * QT, (k + 1) * QT):
                        last = nc.vector.bn_stats(stats[:, n, :], o_sb[:, n, 0:E])
                    last.then_inc(own_dve, 1)
                    dve.wait_ge(own_dve, settled())
                elif kind == "norm":
                    m_e, v_e, m_o, v_o = (stats[:, :, i] for i in (1, 2, 4, 5))
                    s = [small[:, i, :] for i in range(10)]
                    nc.vector.tensor_tensor(s[0], m_e, m_o, ALU.add)
                    nc.vector.tensor_tensor(s[3], v_e, v_o, ALU.add)
                    nc.vector.tensor_tensor(s[1], m_e, m_o, ALU.subtract).then_inc(own_dve, 1)
                    dve.wait_ge(own_dve, settled())
                    nc.vector.tensor_tensor(s[2], s[1], s[1], ALU.mult).then_inc(own_dve, 1)
                    dve.wait_ge(own_dve, settled())
                    nc.vector.scalar_tensor_tensor(out=s[4], in0=s[2], scalar=E / 4.0, in1=s[3],
                                                   op0=ALU.mult, op1=ALU.add).then_inc(own_dve, 1)
                    dve.wait_ge(own_dve, settled())
                    nc.vector.tensor_scalar(s[5], s[4], 1.0 / E, 1e-5, ALU.mult, ALU.add).then_inc(var_done, 1)
                    dve.wait_ge(std_done, g + 1)
                    nc.vector.reciprocal(s[7], s[6]).then_inc(own_dve, 1)
                    dve.wait_ge(own_dve, settled())
                    nc.vector.scalar_tensor_tensor(out=s[8], in0=s[0], scalar=-0.5, in1=s[7],
                                                   op0=ALU.mult, op1=ALU.mult).then_inc(own_dve, 1)
                    dve.wait_ge(own_dve, settled())
                    nc.vector.tensor_tensor(s[3], o_sb[:, :, E], s[7], ALU.mult).then_inc(own_dve, 1)
                    dve.wait_ge(own_dve, settled())
                    nc.vector.scalar_tensor_tensor(out=s[4], in0=s[8], scalar=rsum[:, 0:1], in1=s[3],
                                                   op0=ALU.mult, op1=ALU.add).then_inc(own_dve, 1)
                    dve.wait_ge(own_dve, settled())
                    nc.vector.tensor_scalar(score[:, 0:NT], s[4], rsum[:, 1:2], None,
                                            ALU.add).then_inc(score_done, 1)
                    for n in range(NT):
                        nc.vector.tensor_scalar(o_sb[:, n, 0:E], o_sb[:, n, 0:E], s[7][:, n:n + 1],
                                                s[8][:, n:n + 1], ALU.mult, ALU.add).then_inc(norm_done, 1)
                elif kind == "pick":
                    dve.wait_ge(score_done, g + 1)
                    nc.vector.transpose(score_b[:, :], score[:, :]).then_inc(own_dve, 1)
                    dve.wait_ge(own_dve, settled())
                    dve.wait_ge(consts, 3)
                    other = score_b[:, None, :].to_broadcast([P, T, T])
                    this = score_b[:, :, None].to_broadcast([P, T, T])
                    nc.vector.tensor_tensor(gt[:, :, :], other, this, ALU.is_gt).then_inc(own_dve, 1)
                    dve.wait_ge(own_dve, settled())
                    nc.vector.tensor_tensor(eq[:, :, :], other, this, ALU.is_equal).then_inc(own_dve, 1)
                    dve.wait_ge(own_dve, settled())
                    nc.vector.tensor_tensor(eq[:, :, :], eq[:, :, :], before[:, :, :],
                                            ALU.mult).then_inc(own_dve, 1)
                    dve.wait_ge(own_dve, settled())
                    nc.vector.tensor_tensor(gt[:, :, :], gt[:, :, :], eq[:, :, :], ALU.add).then_inc(own_dve, 1)
                    dve.wait_ge(own_dve, settled())
                    nc.vector.tensor_reduce(rank_b[:, :], gt[:, :, :], AX_X, ALU.add).then_inc(own_dve, 1)
                    dve.wait_ge(own_dve, settled())
                    nc.vector.transpose(rank_n[:, :], rank_b[:, :]).then_inc(own_dve, 1)
                    dve.wait_ge(own_dve, settled())
                    nc.vector.tensor_tensor(pick[:, :, :], rank_of[:, None, :].to_broadcast([P, NT, SEL]),
                                            rank_n[:, 0:NT, None].to_broadcast([P, NT, SEL]),
                                            ALU.is_equal).then_inc(pick_done, 1)
                    dve.wait_ge(sig_done, g + 1)
                    nc.vector.scalar_tensor_tensor(out=weight[:, :], in0=rank_n[:, 0:NT], scalar=float(TOPK),
                                                   in1=small[:, 9, :], op0=ALU.is_lt,
                                                   op1=ALU.mult).then_inc(own_dve, 1)
                    dve.wait_ge(own_dve, settled())
                elif kind == "down":
                    dve.wait_ge(full(step), filled(step))
                    dve.wait_ge(rest_in, REST)
                    nc.vector.tensor_tensor(
                        down[:, :, :], slot(step)[:, :].rearrange("p (n e) -> p n e", e=E),
                        b2_r[:, None, :].to_broadcast([P, NS, E]), ALU.add).then_inc(read(step), 1)
                elif kind == "scatter":
                    dve.wait_ge(full(step), filled(step))
                    dve.wait_ge(res_done, 2 * g + k + 1)
                    for j in range(NT // 2):
                        n = k * NT // 2 + j
                        src = slot(step)[:, j % 2 * BANK + j // 2 * E:][:, 0:E]
                        last = nc.vector.scalar_tensor_tensor(
                            out=x_nat[:, g, n, :], in0=src, scalar=weight[:, n:n + 1], in1=x_nat[:, g, n, :],
                            op0=ALU.mult, op1=ALU.add)
                    last.then_inc(read(step), 1)

        @block.tensor
        def _(pe):
            pe.wait_ge(w_in, W_ALL)
            pe.wait_ge(consts, 1)
            for i, w in enumerate((wg_in[:, 0:E], wg_in[:, E:2 * E], wsoma_in[:, :])):
                nc.tensor.transpose(st_ps[:, 0, i * P:(i + 1) * P], w, ident[:, :])
            nc.tensor.transpose(st_ps[:, 0, 3 * P:3 * P + HN], wn1_in[:, :], ident[0:HN, 0:HN]).then_inc(turned, 1)
            nc.tensor.transpose(st_ps[0:HN, 1, 0:P], wn2_in[:, :], ident[:, :])
            for i, w in enumerate((wtemp_in, wout_in, blend_in)):
                last = nc.tensor.transpose(st_ps[:, 1, (i + 1) * P:(i + 2) * P], w[:, :], ident[:, :])
            last.then_inc(turned, 1)
            pe.wait_ge(tabled, 4)
            nc.tensor.transpose(st_ps[:, 2, 0:P], sexp[:, :], ident[:, :])
            nc.tensor.transpose(st_ps[:, 2, P:2 * P], tail_row[:, :, :].rearrange("p b t -> p (b t)"),
                                ident[:, :]).then_inc(turned, 1)
            pe.wait_ge(consts, 3)
            nc.tensor.matmul(st_ps[:, 3, 0:2], wout_in[:, :], rw[:, :], start=True, stop=True)
            nc.tensor.matmul(st_ps[:, 3, 2:4], ones[:, :], rw[:, :], start=True, stop=True).then_inc(turned, 1)

            for step in STEPS:
                kind, g, k = step
                if step in USE and reads_before(step):
                    pe.wait_ge(read(step), reads_before(step))
                dst = slot(step) if step in USE else None
                blocks = [(slice(k * SLOT + i * BANK, k * SLOT + (i + 1) * BANK),
                           slice(i * BANK, (i + 1) * BANK)) for i in range(2)]
                if kind == "xt":
                    pe.wait_ge(x_in[2 * g + k], 16)
                    for n in range(NT // 2):
                        last = nc.tensor.transpose(dst[:, n * P:(n + 1) * P], x_nat[:, g, k * NT // 2 + n, :],
                                                   ident[:, :])
                elif kind in ("soma", "h1"):
                    for i in range(2):
                        pe.wait_ge(read(("xt", g, i)), reads_after(("xt", g, i)))
                    pe.wait_ge(tabled, 2)
                    w, rows = (wsoma_t, P) if kind == "soma" else (wn1_t, HN)
                    for src, col_ in blocks:
                        last = nc.tensor.matmul(dst[0:rows, col_], w, x_t[:, g, src], start=True, stop=True)
                elif kind == "wg":
                    pe.wait_ge(ctx_done, g + 1)
                    for src, col_ in blocks:
                        nc.tensor.matmul(dst[:, col_], wgx_t, x_t[:, g, src], start=True, stop=False)
                        last = nc.tensor.matmul(dst[:, col_], wgc_t, ctx_acc[:, g, src], start=False, stop=True)
                elif kind == "mod":
                    pe.wait_ge(read(("h1", g, k)), reads_after(("h1", g, k)))
                    for src, col_ in blocks:
                        last = nc.tensor.matmul(dst[:, col_], wn2_t[:, :], h1[:, src], start=True, stop=True)
                elif kind == "nat":
                    pe.wait_ge(gated_done, 2 * g + k // 2 + 1)
                    pe.wait_ge(mod_done, 2 * g + k // 2 + 1)
                    for i, src in enumerate((mod, gated)):
                        for n in range(QT):
                            last = nc.tensor.transpose(dst[:, i * BANK + n * P:i * BANK + (n + 1) * P],
                                                       tile_cols(src, g, k * QT + n), ident[:, :])
                elif kind == "state":
                    q = g * NQ + k
                    pe.wait_ge(read(("nat", g, k)), reads_after(("nat", g, k)))
                    if q:
                        pe.wait_ge(state_read, q)
                    else:
                        pe.wait_ge(tabled, 5)
                    for n in range(QT):
                        for b in range(BT):
                            rows = slice(b * T, b * T + L)
                            last = nc.tensor.matmul(st_ps[:, b, n * E:(n + 1) * E], mod_nat[rows, q % 2, n, :],
                                                    gated_nat[rows, q % 2, n, :], start=True, stop=True)
                    last.then_inc(state_full, 1)
                    continue
                elif kind == "carry":
                    pe.wait_ge(state_read, g * NQ + k + 1)
                    for n in range(QT):
                        for b in range(BT):
                            i = n * BT + b
                            last = nc.tensor.matmul(dst[:, i * L:(i + 1) * L], state[:, b, n, :],
                                                    powers[:, 1:L + 1], start=True, stop=True)
                elif kind == "unit":
                    pe.wait_ge(mod_done, 2 * (g + 1))
                    pe.wait_ge(tabled, 5)
                    to, src = in_slot(dst[:, :], k), lagged(mod[:, g, :], k)
                    for h in range(2):
                        last = nc.tensor.matmul(to[:, h], decayed[:, UNITS[k][0], :], src[:, h],
                                                start=True, stop=True)
                elif kind == "gate":
                    pe.wait_ge(acc_done, (g + 1) * (PER_G + 1))
                    for src, col_ in blocks:
                        last = nc.tensor.matmul(dst[:, col_], wtemp_t[:, :], ctx_acc[:, g, src],
                                                start=True, stop=True)
                elif kind == "out":
                    pe.wait_ge(sg_done, 2 * g + k // 2 + 1)
                    for n in range(QT):
                        at = n // 2 * BANK + n % 2 * OW
                        last = nc.tensor.matmul(dst[:, at:at + OW], tile_cols(x_t, g, k * QT + n),
                                                wout_t[:, :], start=True, stop=True)
                elif kind == "gather":
                    pe.wait_ge(pick_done, g + 1)
                    pe.wait_ge(norm_done, (g + 1) * NT)
                    for n in range(NT):
                        last = nc.tensor.matmul(dst[:, n * SEL:(n + 1) * SEL], o_sb[:, n, 0:E], pick[:, n, :],
                                                start=True, stop=True)
                elif kind == "turn":
                    for n in range(NS):
                        last = nc.tensor.transpose(
                            dst[:, n * P:(n + 1) * P],
                            pick[:, 2 * n:2 * n + 2, :].rearrange("p n k -> p (n k)"), ident[:, :])
                elif kind == "up":
                    pe.wait_ge(read(("gather", g, 0)), reads_after(("gather", g, 0)))
                    pe.wait_ge(rest_in, REST)
                    for i in range(2):
                        last = nc.tensor.matmul(dst[:, i * BANK:(i + 1) * BANK], w1_sb[:, k * P:(k + 1) * P],
                                                hid_t[:, i * BANK:(i + 1) * BANK], start=True, stop=True)
                elif kind == "down":
                    for f in range(NF):
                        pe.wait_ge(read(("up", g, f)), reads_after(("up", g, f)))
                    for n in range(NS):
                        for f in range(NF):
                            src = inner[:, g, f * SLOT + n * P:f * SLOT + (n + 1) * P]
                            last = nc.tensor.matmul(dst[:, n * E:(n + 1) * E], src, w2_sb[:, f, :],
                                                    start=(f == 0), stop=(f == NF - 1))
                elif kind == "scatter":
                    pe.wait_ge(read(("turn", g, 0)), reads_after(("turn", g, 0)))
                    pe.wait_ge(read(("down", g, 0)), reads_after(("down", g, 0)))
                    for j in range(NT // 2):
                        n = k * NT // 2 + j
                        rows = slice(n % 2 * SEL, (n % 2 + 1) * SEL)
                        last = nc.tensor.matmul(dst[:, j % 2 * BANK + j // 2 * E:][:, 0:E],
                                                pick_t[rows, n // 2, :], down[rows, n // 2, :],
                                                start=True, stop=True)
                if step in USE:
                    last.then_inc(full(step), 1)


_INS = ["x", "condB_tauraws", "cond_256", "condB_bn2", "cond_1024", "L0_cond_tau_ctx", "L0_cond_Wg",
        "L0_cond_bg", "L0_cond_Wn1", "L0_cond_bn1", "L0_cond_Wsoma", "L0_cond_bsoma", "L0_cond_Wtemp",
        "L0_cond_btemp", "L0_cond_Wout", "L0_cond_gamma", "L0_cond_beta", "L0_ffn_w_router", "L0_ffn_W1",
        "L0_ffn_b1", "L0_ffn_W2", "L0_ffn_b2"]


def kernel(**inputs):
    import numpy as _np
    import concourse.bacc as _bacc
    from concourse import mybir as _mybir
    from concourse.bass_utils import run_bass_kernel_spmd as _run

    nc = _bacc.Bacc("TRN2", target_bir_lowering=False, num_devices=1)
    arrays, args = {}, []
    for name in _INS:
        a = _np.ascontiguousarray(inputs[name])
        if name == "L0_cond_tau_ctx":
            a = a.reshape(1, 1)
        arrays[f"in_{name}_dram"] = a
        args.append(nc.dram_tensor(f"in_{name}_dram", a.shape, _mybir.dt.from_np(a.dtype), kind="ExternalInput").ap())
    args.append(nc.dram_tensor("out_0_dram", (B, T, E), _mybir.dt.from_np(_np.dtype("float32")),
                               kind="ExternalOutput").ap())
    adaln_ffn(nc, *args)
    r = _run(nc, [arrays], core_ids=[0])
    return r.results[0]["out_0_dram"]
```

```python
from contextlib import ExitStack

import concourse.bass as bass
from concourse import mybir

P = 128
B, T, E, D, F, HN = 128, 32, 128, 128, 512, 32
TOPK = T // 2
L = T // 2
NCH = T // L
BT = P // T
QT = 4
BQ = BT * QT
QUADS = (1, 2, 2, 2, 1)
BEFORE = tuple(sum(QUADS[:r]) for r in range(len(QUADS) + 1))
R = len(QUADS)
assert BEFORE[R] * BQ == B
NQ = max(QUADS)
NT = NQ * QT
COLS = NT * P
BR = NQ * BQ
SEL = BT * TOPK
NSEL = NT * SEL
NS = NSEL // P
NF = F // P
BANK = 512
SLOT = 2 * BANK
NSLOT = 4
OW = E + 2
NP = 3

ALU = mybir.AluOpType
ACT = mybir.ActivationFunctionType
AX_X = mybir.AxisListType.X
F32 = mybir.dt.float32
F32R = mybir.dt.float32r
BF16 = mybir.dt.bfloat16

REST = 6 * 16
WB = 7 * 16


def tiles(r):
    return QUADS[r] * QT

ORDER = """
turn_a:0 xt:0 decay:0 soma:0 context:0 h1:0 turn_b:0 xt:1 alpha:0 turn_c:0 wg:0 mod:0 turn_d:0 tables:0
context:1 split:0 nat:0 unit:0.0 h1:1 unit:0.12 unit:0.1 unit:0.15 unit:0.2 wg:1 state:0 unit:0.13 mod:1
unit:0.3 soma:1 xt:2 unit:0.14 carry:0 context:2 unit:0.4 unit:0.11 soma:2 unit:0.5 unit:0.10 h1:2
unit:0.6 unit:0.9 wg:2 unit:0.7 unit:0.8 split:1 mod:2 nat:1 sum:0 xt:3 nat:1.1 unit:1.0 context:3
unit:1.12 h1:3 soma:3 unit:1.1 unit:1.15 wg:3 mod:3 state:1 xt:4 unit:1.2 unit:1.13 soma:4 context:4
unit:1.3 h1:4 unit:1.14 wg:4 carry:1 unit:1.4 mod:4 unit:1.11 gate:0 state:1.1 out:0 unit:1.5 var:0
unit:1.10 score:0 unit:1.6 rank:0 normed:0 carry:1.1 unit:1.9 unit:1.7 rank:0.1 residual:0 unit:1.8
pick:0 sum:1 split:2 gather:0 nat:2 up:0 unit:2.0 unit:2.12 unit:2.1 up:0.1 unit:2.15 down:0 scatter:0
state:2 gate:1 unit:2.2 out:1 unit:2.13 out:1.1 unit:2.3 var:1 nat:2.1 carry:2 unit:2.14 score:1 rank:1
normed:1 unit:2.4 rank:1.1 unit:2.11 residual:1 state:2.1 unit:2.5 unit:2.10 pick:1 unit:2.6 gather:1
carry:2.1 up:1 unit:2.9 split:3 up:1.1 unit:2.7 unit:2.8 sum:2 down:1 nat:3 scatter:1 unit:3.0 unit:3.12
gate:2 unit:3.1 out:2 unit:3.15 out:2.1 state:3 unit:3.2 var:2 unit:3.13 score:2 unit:3.3 nat:3.1 rank:2
unit:3.14 carry:3 unit:3.4 normed:2 unit:3.11 rank:2.1 pick:2 unit:3.5 state:3.1 gather:2 unit:3.10
unit:3.6 up:2 carry:3.1 unit:3.9 up:2.1 residual:2 unit:3.7 split:4 down:2 unit:3.8 sum:3 scatter:2
nat:4 unit:4.0 gate:3 unit:4.12 out:3 unit:4.1 unit:4.15 state:4 out:3.1 var:3 unit:4.2 unit:4.13
score:3 unit:4.3 rank:3 unit:4.14 carry:4 rank:3.1 unit:4.4 unit:4.11 normed:3 pick:3 unit:4.5 unit:4.10
unit:4.6 gather:3 up:3 residual:3 unit:4.9 up:3.1 unit:4.7 unit:4.8 sum:4 down:3 scatter:3 gate:4 out:4
var:4 score:4 rank:4 normed:4 rank:4.1 pick:4 gather:4 residual:4 up:4 up:4.1 down:4 scatter:4
"""


def parsed(word):
    kind, _, at = word.partition(":")
    r, _, k = at.partition(".")
    return kind, int(r), int(k or 0)


STEPS = [parsed(word) for word in ORDER.split()]

QUAD = [(r, k) for r in range(R) for k in range(QUADS[r])]

READERS = {"turn_a": 2, "turn_b": 2, "turn_c": 2, "turn_d": 2, "xt": 1, "soma": 1, "h1": 1, "wg": 1, "mod": 1,
           "nat": 2, "state": 1, "carry": 1, "unit": 1, "gate": 1, "out": 1, "gather": 2, "up": 2, "down": 1,
           "scatter": 1}
RING = [(s, i) for s in STEPS if s[0] in READERS for i in range(2 if s[0] == "state" else 1)]
USE = {u: n for n, u in enumerate(RING)}


def filled(step, i=0):
    return USE[step, i] // NSLOT + 1


def reads_before(step, i=0):
    n = USE[step, i]
    return sum(READERS[s[0]] for s, _ in RING[n % NSLOT:n:NSLOT])


def reads_after(step, i=0):
    return reads_before(step, i) + READERS[step[0]]


H1_LAST = {r % 2: r for kind, r, k in STEPS if kind == "mod"}
assert all(STEPS.index(("mod", r, 0)) < STEPS.index(("out", p, 0)) for p, r in H1_LAST.items())
assert max(STEPS.index(("context", r, 0)) for r in range(R)) < STEPS.index(("rank", 0, 0))


def adaln_ffn(nc, x, tau_raws, w_n2, b_n2, blend, tau_ctx, w_g, b_g, w_n1, b_n1, w_soma, b_soma,
              w_temp, b_temp, w_out, gamma, beta, w_router, w_1, b_1, w_2, b_2, out):
    with ExitStack() as ctx:
        def sb(name, shape, dt=F32):
            return ctx.enter_context(nc.sbuf_tensor(name, shape, dt))

        def sem(name):
            return ctx.enter_context(nc.semaphore(name))

        ring = ctx.enter_context(nc.psum_tensor("ring", [P, NSLOT, SLOT], F32))

        ident = sb("ident", [P, P])
        ones = sb("ones", [P, P])
        wg_in = sb("wg_in", [P, 2 * E])
        wn1_in = sb("wn1_in", [HN, E])
        wn2_in = sb("wn2_in", [P, HN])
        blend_in = sb("blend_in", [P, E])
        wsoma_in = sb("wsoma_in", [P, E])
        wtemp_in = sb("wtemp_in", [P, E])
        wout_in = sb("wout_in", [P, E])
        w1_sb = sb("w1_sb", [P, F])
        w2_sb = sb("w2_sb", [P, NF, E])
        turned_w = sb("turned_w", [P, 3 * P + HN])
        wgx_t, wgc_t, wsoma_t = (turned_w[:, i * P:(i + 1) * P] for i in range(3))
        wn1_t = turned_w[:, 3 * P:3 * P + HN]
        wn2_t = sb("wn2_t", [HN, D])
        wtemp_t = sb("wtemp_t", [P, E])
        wout_t = sb("wout_t", [P, OW])
        bg, bsoma, btemp = sb("bg", [P, 1]), sb("bsoma", [P, 1]), sb("btemp", [P, 1])
        bn1, bn2 = sb("bn1", [HN, 1]), sb("bn2", [P, 1])
        gamma_c, beta_c, router = sb("gamma_c", [P, 1]), sb("beta_c", [P, 1]), sb("router", [P, 1])
        b1_c = sb("b1_c", [P, NF])
        gamma_r, beta_r, b2_r = sb("gamma_r", [P, E]), sb("beta_r", [P, E]), sb("b2_r", [P, E])
        taus = sb("taus", [P, 2])
        tau_e, tau_s, alphas = sb("tau_e", [P, 2]), sb("tau_s", [P, 2]), sb("alphas", [P, 2])
        alpha, alpha_ctx = alphas[:, 0:1], alphas[:, 1:2]
        warm = sb("warm", [P, 1])
        smax, ssum, srec = sb("smax", [P, 1]), sb("ssum", [P, 1]), sb("srec", [P, 1])
        sexp = sb("sexp", [P, P])
        blend_t = sb("blend_t", [P, P])
        blend_w = sb("blend_w", [P, E])
        decayed_hi, decayed_lo = sb("decayed_hi", [P, L, E], F32R), sb("decayed_lo", [P, L, E], F32R)
        powers = sb("powers", [P, L + 1])
        tail_row = sb("tail_row", [P, BT, T])
        tail = sb("tail", [P, D])
        rw = sb("rw", [P, 2])
        rsum = sb("rsum", [P, 2])
        rank_of = sb("rank_of", [P, SEL])
        before = sb("before", [P, T, T], BF16)

        x_nat = sb("x_nat", [P, B // BT, E])
        x_t = sb("x_t", [P, B * T])
        ctx_acc = sb("ctx_acc", [P, B * T])
        gm = sb("gm", [P, 2 * B * T])
        soma = sb("soma", [P, B * T])
        mod_hi, mod_lo = sb("mod_hi", [P, 2, COLS], F32R), sb("mod_lo", [P, 2, COLS], F32R)
        mod_nat = sb("mod_nat", [P, 2, QT, D])
        gated_nat = sb("gated_nat", [P, 2, QT, E])
        state = sb("state", [P, BT, QT, E])
        carried = sb("carried", [P, 2, BR, L])
        prod = sb("prod", [P, NP, SLOT])
        prod_res = sb("prod_res", [P, NT, E])
        o_sb = sb("o_sb", [P, 2, NT, OW])
        stats = sb("stats", [P, NT, 6])
        small = sb("small", [P, 10, NT])
        score = sb("score", [P, T])
        score_b = sb("score_b", [P, T])
        compared = sb("compared", [P, 2, T, T], BF16)
        gt, eq = compared[:, 0], compared[:, 1]
        ctx_decay = compared[:, :, :, :].rearrange("p i t u -> p (i t u)").bitcast(F32)
        rank_b = sb("rank_b", [P, T])
        rank_n = sb("rank_n", [P, T])
        weight = sb("weight", [P, 2, NT])
        pick = sb("pick", [P, NT, SEL])
        pick_t = sb("pick_t", [P, NS, P])
        hid_t = sb("hid_t", [P, NSEL])
        down = sb("down", [P, NS, E])
        h1 = o_sb[0:HN].rearrange("p i n w -> p i (n w)")[:, :, 0:COLS]
        decayed = state[:, :, :, :].rearrange("p b n e -> p (b n) e")

        x_in = [sem(f"x_in{r}") for r in range(R)]
        wa_in, ba_in, tau_in, wb_in, rest_in = (sem(n) for n in ("wa_in", "ba_in", "tau_in", "wb_in", "rest_in"))
        own_pool, own_dve = sem("own_pool"), sem("own_dve")
        consts = sem("consts")
        alphas_done = sem("alphas_done")
        exped = sem("exped")
        tabled = sem("tabled")
        slot_full = [sem(f"slot_full{i}") for i in range(NSLOT)]
        slot_read = [sem(f"slot_read{i}") for i in range(NSLOT)]
        ctx_done = sem("ctx_done")
        gated_done, split_done = sem("gated_done"), sem("split_done")
        hi_done = sem("hi_done")
        acc_done = sem("acc_done")
        sg_done = sem("sg_done")
        var_done, std_done = sem("var_done"), sem("std_done")
        norm_done = sem("norm_done")
        score_done, sig_done = sem("score_done"), sem("sig_done")
        pick_done = sem("pick_done")
        res_done, xb_done = sem("res_done"), sem("xb_done")
        y_out = sem("y_out")

        x_dram = x.rearrange("b t e -> (b t) e").rearrange("(n p) e -> p n e", p=P)
        y_dram = out.rearrange("b t e -> (b t) e").rearrange("(n p) e -> p n e", p=P)

        def col(v):
            return v.rearrange("(p o) -> p o", o=1)

        def row(v):
            return v.rearrange("(o n) -> o n", o=1).to_broadcast([P, v.shape[0]])

        def slot(step, i=0):
            return ring[:, USE[step, i] % NSLOT, :]

        def cols_of(step):
            return slot(step)[:, 0:tiles(step[1]) * P]

        def full(step, i=0):
            return slot_full[USE[step, i] % NSLOT]

        def read(step, i=0):
            return slot_read[USE[step, i] % NSLOT]

        def tiles_of(buf, r):
            return buf[:, BEFORE[r] * QT:BEFORE[r + 1] * QT]

        def part(buf, r, first=0, last=None):
            last = tiles(r) * P if last is None else last
            return buf[:, BEFORE[r] * BANK + first:BEFORE[r] * BANK + last]

        def gated(r):
            return gm[:, 2 * BEFORE[r] * BANK:][:, 0:QUADS[r] * BANK]

        def sig(r):
            return gm[:, (2 * BEFORE[r] + QUADS[r]) * BANK:][:, 0:QUADS[r] * BANK]

        def inner(r, first, last):
            return gm[:, 2 * BEFORE[r] * BANK + first:2 * BEFORE[r] * BANK + last]

        def lagged(buf, r, lag, shift=0):
            t0 = shift * lag
            return buf.rearrange("p (h b t) -> p h t b", h=QUADS[r], t=L)[:, :, t0:t0 + L - lag, :]

        def in_slot(buf, r, lag):
            n = (L - lag) * NCH * BQ
            return buf[:, 0:QUADS[r] * BANK].rearrange("p (h n) -> p h n", h=QUADS[r])[:, :, 0:n].rearrange(
                "p h (t b) -> p h t b", t=L - lag)


        LAGS = [k for kind, r, k in STEPS if kind == "unit" and r == 0]
        assert LAGS[0] == 0

        def sums_to(r, i):
            return r * L + i

        block = ctx.enter_context(nc.Block())

        @block.sync
        def _(sp):
            sp.dma_start(tiles_of(x_nat, 0), tiles_of(x_dram, 0)).then_inc(x_in[0], 16)
            sp.dma_start(wn1_in[:, :], w_n1).then_inc(wa_in, 16)
            sp.dma_start(wn2_in[:, :], w_n2).then_inc(wa_in, 16)
            sp.dma_start(taus[:, 1:2], tau_ctx.to_broadcast([P, 1])).then_inc(tau_in, 16)
            sp.dma_start(tiles_of(x_nat, 1), tiles_of(x_dram, 1)).then_inc(x_in[1], 16)
            sp.dma_start(bg[:, :], col(b_g)).then_inc(ba_in, 16)
            sp.dma_start(bn2[:, :], col(b_n2)).then_inc(ba_in, 16)
            sp.dma_start(tiles_of(x_nat, 2), tiles_of(x_dram, 2)).then_inc(x_in[2], 16)
            sp.dma_start(tiles_of(x_nat, 3), tiles_of(x_dram, 3)).then_inc(x_in[3], 16)
            sp.dma_start(tiles_of(x_nat, 4), tiles_of(x_dram, 4)).then_inc(x_in[4], 16)
            sp.dma_start(w1_sb[:, :], w_1).then_inc(rest_in, 16)
            sp.dma_start(w2_sb[:, :, :], w_2.rearrange("(k p) e -> p k e", p=P)).then_inc(rest_in, 16)
            sp.dma_start(b1_c[:, :], b_1.rearrange("(k p) -> p k", p=P),
                         allow_slow_non_contiguous=True).then_inc(rest_in, 16)
            sp.dma_start(gamma_r[:, :], row(gamma)).then_inc(rest_in, 16)
            sp.dma_start(beta_r[:, :], row(beta)).then_inc(rest_in, 16)
            sp.dma_start(b2_r[:, :], row(b_2)).then_inc(rest_in, 16)
            for r in range(R):
                step = ("scatter", r, 0)
                sp.wait_ge(read(step), reads_after(step))
                sp.dma_start(tiles_of(y_dram, r), tiles_of(x_nat, r)).then_inc(y_out, 16)
            sp.wait_ge(y_out, R * 16)

        @block.gpsimd
        def _(pool):
            nc.gpsimd.memset(ident[:, :], 0.0).then_inc(own_pool, 1)
            nc.gpsimd.memset(ones[:, :], 1.0).then_inc(own_pool, 1)
            pool.wait_ge(own_pool, 2)
            nc.gpsimd.affine_select(out=ident[:, :], in_=ident[:, :], compare_op=ALU.not_equal, fill=1.0,
                                    base=0, pattern=[[-1, P]], channel_multiplier=1).then_inc(consts, 1)
            nc.gpsimd.memset(before[:, :, :], 1.0).then_inc(own_pool, 1)
            nc.gpsimd.iota(rank_of[:, :], pattern=[[0, BT], [1, TOPK]], base=0, channel_multiplier=0,
                           allow_small_or_imprecise_dtypes=True).then_inc(own_pool, 1)
            pool.wait_ge(own_pool, 4)
            places = rank_of[:, :].rearrange("p (b j) -> p b j", b=BT)
            nc.gpsimd.affine_select(out=places, in_=places, compare_op=ALU.is_ge, fill=-1.0, base=0,
                                    pattern=[[-T, BT], [0, TOPK]], channel_multiplier=1).then_inc(own_pool, 1)
            pool.wait_ge(own_pool, 5)
            nc.gpsimd.affine_select(out=places, in_=places, compare_op=ALU.is_ge, fill=-1.0, base=T - 1,
                                    pattern=[[T, BT], [0, TOPK]], channel_multiplier=-1).then_inc(consts, 1)
            nc.gpsimd.affine_select(out=before[:, :, :], in_=before[:, :, :], compare_op=ALU.is_ge, fill=0.0,
                                    base=-1, pattern=[[1, T], [-1, T]], channel_multiplier=0).then_inc(consts, 1)
            pool.wait_ge(rest_in, REST)
            for step in STEPS:
                kind, r, k = step
                if kind == "xt":
                    pool.wait_ge(read(step), reads_after(step))
                    x_r = tiles_of(x_nat, r)
                    nc.gpsimd.tensor_tensor(x_r, x_r, beta_r[:, None, :].to_broadcast([P, tiles(r), E]),
                                            ALU.add).then_inc(xb_done, 1)
                elif kind == "unit" and k > 0:
                    i = LAGS.index(k)
                    n = r * (L - 1) + i - 1
                    dst = lagged(part(ctx_acc, r), r, k, shift=1)
                    pool.wait_ge(read(step), reads_after(step))
                    if i > 1:
                        pool.wait_ge(acc_done, sums_to(r, i - 1))
                    nc.gpsimd.tensor_tensor(dst, dst, in_slot(prod[:, n % NP, :], r, k), ALU.add).then_inc(acc_done, 1)
                elif kind == "sum":
                    for q in range(QUADS[r]):
                        pool.wait_ge(read(("carry", r, q)), reads_after(("carry", r, q)))
                    pool.wait_ge(acc_done, sums_to(r, L - 1))
                    dst = part(ctx_acc, r).rearrange("p (b t) -> p b t", t=T)[:, :, L:]
                    nc.gpsimd.tensor_tensor(dst, dst, carried[:, r % 2, 0:QUADS[r] * BQ], ALU.add).then_inc(acc_done, 1)
                elif kind == "residual":
                    pool.wait_ge(norm_done, BEFORE[r + 1] * QT)
                    if r:
                        pool.wait_ge(res_done, r)
                    nc.gpsimd.tensor_tensor(prod_res[:, 0:tiles(r), :], o_sb[:, r % 2, 0:tiles(r), 0:E],
                                            gamma_r[:, None, :].to_broadcast([P, tiles(r), E]),
                                            ALU.mult).then_inc(own_pool, 1)
                    pool.wait_ge(own_pool, 6 + r)
                    pool.wait_ge(xb_done, r + 1)
                    nc.gpsimd.tensor_tensor(tiles_of(x_nat, r), tiles_of(x_nat, r), prod_res[:, 0:tiles(r), :],
                                            ALU.add).then_inc(res_done, 1)

        @block.scalar
        def _(act):
            act.dma_start(wg_in[:, :], w_g).then_inc(wa_in, 16)
            act.dma_start(taus[:, 0:1], col(tau_raws)).then_inc(tau_in, 16)
            act.dma_start(wsoma_in[:, :], w_soma).then_inc(wa_in, 16)
            act.dma_start(bsoma[:, :], col(b_soma)).then_inc(ba_in, 16)
            act.dma_start(bn1[:, :], col(b_n1)).then_inc(ba_in, 16)
            for dst, src in ((blend_in[:, :], blend), (wtemp_in[:, :], w_temp), (wout_in[:, :], w_out),
                             (btemp[:, :], col(b_temp)), (gamma_c[:, :], col(gamma)), (beta_c[:, :], col(beta)),
                             (router[:, :], col(w_router))):
                act.dma_start(dst, src).then_inc(wb_in, 16)
            for step in STEPS:
                kind, r, k = step
                if kind in ("xt", "soma", "h1", "wg", "mod", "nat", "carry", "gate", "out", "gather", "up"):
                    act.wait_ge(full(step), filled(step))
                if kind == "decay":
                    act.wait_ge(tau_in, 2 * 16)
                    nc.scalar.activation(tau_e[:, :], taus[:, :], ACT.Exp).then_inc(exped, 1)
                    act.wait_ge(ba_in, 4 * 16)
                elif kind == "turn_b":
                    act.wait_ge(alphas_done, 2)
                    nc.scalar.activation(sexp[:, :], blend_t[:, :], ACT.Exp, bias=smax[:, :],
                                         accum_out=ssum[:, :]).then_inc(exped, 1)
                elif kind == "turn_d":
                    act.wait_ge(wb_in, WB)
                elif kind == "xt":
                    nc.scalar.activation(part(x_t, r), cols_of(step), ACT.Copy).then_inc(read(step), 1)
                elif kind == "soma":
                    nc.scalar.activation(part(soma, r), cols_of(step), ACT.Gelu,
                                         bias=bsoma[:, :]).then_inc(read(step), 1)
                elif kind == "h1":
                    if r >= 2:
                        last = ("mod", r - 2, 0)
                        act.wait_ge(full(last), filled(last))
                    nc.scalar.activation(h1[:, r % 2, 0:tiles(r) * P], cols_of(step)[0:HN], ACT.Gelu,
                                         bias=bn1[:, :]).then_inc(read(step), 1)
                elif kind == "wg":
                    nc.scalar.activation(gated(r), cols_of(step), ACT.Sigmoid, bias=bg[:, :]).then_inc(read(step), 1)
                elif kind == "mod":
                    nc.scalar.activation(sig(r), cols_of(step), ACT.Sigmoid, bias=bn2[:, :]).then_inc(read(step), 1)
                elif kind == "split":
                    act.wait_ge(read(("mod", r, 0)), reads_after(("mod", r, 0)))
                    if r >= 2:
                        last = ("unit", r - 2, LAGS[-1])
                        act.wait_ge(full(last), filled(last))
                    nc.scalar.activation(mod_hi[:, r % 2, 0:tiles(r) * P], sig(r), ACT.Copy,
                                         bias=0.5).then_inc(hi_done, 1)
                elif kind == "nat":
                    q = BEFORE[r] + k
                    if q >= 2:
                        last = ("state", *QUAD[q - 2])
                        act.wait_ge(full(last, 1), filled(last, 1))
                    nc.scalar.activation(gated_nat[:, q % 2, :, :].rearrange("p n e -> p (n e)"),
                                         slot(step)[:, BANK:], ACT.Copy).then_inc(read(step), 1)
                elif kind == "carry":
                    if r >= 2 and k == 0:
                        act.wait_ge(acc_done, sums_to(r - 1, 0))
                    dst = carried[:, r % 2, k * BQ:(k + 1) * BQ, :].rearrange("p b t -> p (b t)")
                    nc.scalar.activation(dst, slot(step)[:, 0:BQ * L], ACT.Copy).then_inc(read(step), 1)
                elif kind == "gate":
                    nc.scalar.activation(part(x_t, r), cols_of(step), ACT.Sigmoid,
                                         bias=btemp[:, :]).then_inc(read(step), 1)
                elif kind == "out":
                    if r < 2 and k == 0:
                        last = ("mod", H1_LAST[r], 0)
                        act.wait_ge(full(last), filled(last))
                    elif k == 0:
                        last = ("gather", r - 2, 0)
                        act.wait_ge(res_done, r - 1)
                        act.wait_ge(full(last), filled(last))
                    src = slot(step).rearrange("p (h n) -> p h n", h=2)[:, :, 0:2 * OW]
                    dst = o_sb[:, r % 2, k * QT:(k + 1) * QT, :].rearrange("p (h n) w -> p h (n w)", h=2)
                    nc.scalar.activation(dst, src, ACT.Copy).then_inc(read(step), 1)
                elif kind == "var":
                    nc.scalar.activation(warm[:, :], ones[:, 0:1], ACT.Sqrt)
                    act.wait_ge(var_done, r + 1)
                    nc.scalar.activation(small[:, 6, 0:tiles(r)], small[:, 5, 0:tiles(r)], ACT.Sqrt).then_inc(std_done, 1)
                elif kind == "normed":
                    act.wait_ge(score_done, r + 1)
                    for n in range(tiles(r)):
                        nc.scalar.activation(o_sb[:, r % 2, n, 0:E], o_sb[:, r % 2, n, 0:E], ACT.Identity,
                                             bias=small[:, 8, n:n + 1],
                                             scale=small[:, 7, n:n + 1]).then_inc(norm_done, 1)
                    nc.scalar.activation(small[:, 9, 0:tiles(r)], score[:, 0:tiles(r)], ACT.Tanh,
                                         scale=0.5).then_inc(sig_done, 1)
                elif kind == "gather":
                    nc.scalar.activation(hid_t[:, 0:tiles(r) * SEL], slot(step)[:, 0:tiles(r) * SEL], ACT.Identity, bias=beta_c[:, :],
                                         scale=gamma_c[:, :]).then_inc(read(step), 1)
                    nc.scalar.activation(pick_t[:, 0:tiles(r) // 2, :].rearrange("p n k -> p (n k)"),
                                         slot(step)[:, BANK:BANK + tiles(r) // 2 * P],
                                         ACT.Copy).then_inc(read(step), 1)
                elif kind == "up":
                    if r == 0 and k == 0:
                        act.wait_ge(rest_in, REST)
                    n_sel = tiles(r) * SEL
                    for i in range(2):
                        f = 2 * k + i
                        nc.scalar.activation(inner(r, f * n_sel, (f + 1) * n_sel),
                                             slot(step)[:, i * BANK:i * BANK + n_sel], ACT.Gelu_apprx_tanh,
                                             bias=b1_c[:, f:f + 1]).then_inc(read(step), 1)

        @block.vector
        def _(dve):
            own = [0]

            def settled():
                own[0] += 1
                return own[0]

            nc.vector.memset(powers[:, 0:1], 1.0)
            nc.vector.memset(score[:, :], 0.0)
            nc.vector.memset(tail_row[:, :, :], 1.0).then_inc(own_dve, 1)
            dve.wait_ge(own_dve, settled())
            for step in STEPS:
                kind, r, k = step
                if kind in ("turn_a", "turn_b", "turn_c", "turn_d", "nat", "unit", "down", "scatter"):
                    dve.wait_ge(full(step), filled(step))
                if kind == "turn_a":
                    nc.vector.tensor_copy(turned_w[:, :], slot(step)[:, 0:3 * P + HN]).then_inc(read(step), 1)
                    nc.vector.tensor_copy(wn2_t[:, :], slot(step)[0:HN, BANK:BANK + P]).then_inc(read(step), 1)
                elif kind == "decay":
                    dve.wait_ge(exped, 1)
                    nc.vector.tensor_scalar(tau_s[:, :], tau_e[:, :], 1.0, None, ALU.add).then_inc(own_dve, 1)
                    dve.wait_ge(own_dve, settled())
                    nc.vector.reciprocal(alphas[:, :], tau_s[:, :]).then_inc(own_dve, 1)
                    dve.wait_ge(own_dve, settled())
                    nc.vector.tensor_copy(ctx_decay, alpha_ctx.to_broadcast([P, COLS])).then_inc(own_dve, 1)
                    dve.wait_ge(own_dve, settled())
                    nc.vector.memset(ctx_decay.rearrange("p (b t) -> p b t", t=T)[:, :, 0:1],
                                     0.0).then_inc(alphas_done, 1)
                elif kind == "turn_b":
                    nc.vector.tensor_copy(blend_t[:, :], slot(step)[:, 0:P]).then_inc(own_dve, 1)
                    dve.wait_ge(own_dve, settled())
                    nc.vector.tensor_reduce(smax[:, :], blend_t[:, :], AX_X, ALU.max,
                                            negate=True).then_inc(alphas_done, 1)
                    nc.vector.tensor_copy(wtemp_t[:, :], slot(step)[:, P:2 * P]).then_inc(read(step), 1)
                    nc.vector.tensor_copy(wout_t[:, 0:E], slot(step)[:, 2 * P:3 * P]).then_inc(read(step), 1)
                elif kind == "alpha":
                    dve.wait_ge(alphas_done, 1)
                    dve.wait_ge(consts, 1)
                    nc.vector.tensor_tensor_scan(powers[:, 1:L + 1], alpha.to_broadcast([P, L]), ones[:, 0:L], 1.0,
                                                 ALU.mult, ALU.mult).then_inc(own_dve, 1)
                    dve.wait_ge(own_dve, settled())
                    for t in range(L):
                        nc.vector.tensor_copy(tail_row[:, :, t:t + 1],
                                              powers[:, None, L - 1 - t:L - t].to_broadcast([P, BT, 1]))
                    dve.wait_ge(exped, 2)
                    nc.vector.reciprocal(srec[:, :], ssum[:, :]).then_inc(own_dve, 1)
                    dve.wait_ge(own_dve, settled())
                    nc.vector.tensor_scalar(sexp[:, :], sexp[:, :], srec[:, :], None, ALU.mult).then_inc(tabled, 1)
                    dve.wait_ge(wb_in, WB)
                    nc.vector.tensor_tensor(rw[:, 0:1], gamma_c[:, :], router[:, :], ALU.mult)
                    nc.vector.tensor_tensor(rw[:, 1:2], beta_c[:, :], router[:, :], ALU.mult).then_inc(tabled, 1)
                elif kind == "turn_c":
                    nc.vector.tensor_copy(blend_w[:, :], slot(step)[:, 0:P]).then_inc(read(step), 1)
                    nc.vector.tensor_copy(tail[:, :], slot(step)[:, P:2 * P]).then_inc(read(step), 1)
                elif kind == "tables":
                    turned = ("turn_c", 0, 0)
                    dve.wait_ge(read(turned), reads_after(turned))
                    nc.vector.tensor_tensor(decayed, blend_w[:, None, :].to_broadcast([P, L, E]),
                                            powers[:, 0:L, None].to_broadcast([P, L, E]),
                                            ALU.mult).then_inc(own_dve, 1)
                    dve.wait_ge(own_dve, settled())
                    nc.vector.tensor_copy(decayed_hi[:, :, :], decayed).then_inc(own_dve, 1)
                    dve.wait_ge(own_dve, settled())
                    nc.vector.tensor_tensor(decayed_lo[:, :, :], decayed, decayed_hi[:, :, :].bitcast(F32),
                                            ALU.subtract).then_inc(tabled, 1)
                elif kind == "turn_d":
                    nc.vector.tensor_copy(wout_t[:, E:E + 2], slot(step)[:, 0:2]).then_inc(read(step), 1)
                    nc.vector.tensor_copy(rsum[:, :], slot(step)[:, 2:4]).then_inc(read(step), 1)
                elif kind == "context":
                    dve.wait_ge(alphas_done, 1)
                    dve.wait_ge(read(("xt", r, 0)), reads_after(("xt", r, 0)))
                    nc.vector.tensor_tensor_scan(part(ctx_acc, r), ctx_decay[:, 0:tiles(r) * P], part(x_t, r), 0.0, ALU.mult,
                                                 ALU.add).then_inc(ctx_done, 1)
                elif kind == "wg":
                    dve.wait_ge(read(step), reads_after(step))
                    nc.vector.tensor_tensor(gated(r), gated(r), part(x_t, r),
                                            ALU.mult).then_inc(gated_done, 1)
                elif kind == "split":
                    dve.wait_ge(read(("mod", r, 0)), reads_after(("mod", r, 0)))
                    if r >= 2:
                        last = ("unit", r - 2, LAGS[-1])
                        dve.wait_ge(full(last), filled(last))
                    dve.wait_ge(hi_done, r + 1)
                    nc.vector.scalar_tensor_tensor(
                        out=mod_lo[:, r % 2, 0:tiles(r) * P], in0=sig(r), scalar=0.5,
                        in1=mod_hi[:, r % 2, 0:tiles(r) * P].bitcast(F32), op0=ALU.add, op1=ALU.subtract).then_inc(split_done, 1)
                elif kind == "nat":
                    q = BEFORE[r] + k
                    if q >= 2:
                        last = ("state", *QUAD[q - 2])
                        dve.wait_ge(full(last, 1), filled(last, 1))
                    nc.vector.scalar_tensor_tensor(
                        out=mod_nat[:, q % 2], in0=slot(step)[:, 0:BANK].rearrange("p (n d) -> p n d", n=QT),
                        scalar=0.5, in1=tail[:, None, :].to_broadcast([P, QT, D]), op0=ALU.add,
                        op1=ALU.mult).then_inc(read(step), 1)
                elif kind == "state":
                    q = BEFORE[r] + k
                    if q:
                        last = ("carry", *QUAD[q - 1])
                        dve.wait_ge(full(last), filled(last))
                    for i in range(2):
                        dve.wait_ge(full(step, i), filled(step, i))
                        nc.vector.tensor_tensor(
                            state[:, 2 * i:2 * i + 2].rearrange("p b n e -> p (b n) e"),
                            slot(step, i).rearrange("p (n e) -> p n e", e=E),
                            blend_w[:, None, :].to_broadcast([P, 2 * QT, E]), ALU.mult).then_inc(read(step, i), 1)
                elif kind == "unit":
                    dve.wait_ge(gated_done, r + 1)
                    if k:
                        n = r * (L - 1) + LAGS.index(k) - 1
                        if n >= NP:
                            m = n - NP
                            dve.wait_ge(acc_done, sums_to(m // (L - 1), m % (L - 1) + 1))
                        dst = in_slot(prod[:, n % NP, :], r, k)
                    else:
                        dst = lagged(part(ctx_acc, r), r, 0)
                    nc.vector.tensor_tensor(dst, in_slot(slot(step), r, k), lagged(gated(r), r, k),
                                            ALU.mult).then_inc(read(step), 1)
                elif kind == "gate":
                    dve.wait_ge(read(step), reads_after(step))
                    nc.vector.tensor_tensor(part(x_t, r), part(x_t, r), part(soma, r),
                                            ALU.mult).then_inc(sg_done, 1)
                elif kind == "out":
                    dve.wait_ge(read(step), reads_after(step))
                    for n in range(k * QT, (k + 1) * QT):
                        last = nc.vector.bn_stats(stats[:, n, :], o_sb[:, r % 2, n, 0:E])
                    last.then_inc(own_dve, 1)
                    dve.wait_ge(own_dve, settled())
                elif kind == "var":
                    s = [small[:, i, 0:tiles(r)] for i in range(10)]
                    m_e, v_e, m_o, v_o = (stats[:, 0:tiles(r), i] for i in (1, 2, 4, 5))
                    nc.vector.tensor_tensor(s[0], m_e, m_o, ALU.add)
                    nc.vector.tensor_tensor(s[3], v_e, v_o, ALU.add)
                    nc.vector.tensor_tensor(s[1], m_e, m_o, ALU.subtract).then_inc(own_dve, 1)
                    dve.wait_ge(own_dve, settled())
                    nc.vector.tensor_tensor(s[2], s[1], s[1], ALU.mult).then_inc(own_dve, 1)
                    dve.wait_ge(own_dve, settled())
                    nc.vector.scalar_tensor_tensor(out=s[4], in0=s[2], scalar=E / 4.0, in1=s[3],
                                                   op0=ALU.mult, op1=ALU.add).then_inc(own_dve, 1)
                    dve.wait_ge(own_dve, settled())
                    nc.vector.tensor_scalar(s[5], s[4], 1.0 / E, 1e-5, ALU.mult, ALU.add).then_inc(var_done, 1)
                elif kind == "score":
                    dve.wait_ge(std_done, r + 1)
                    s = [small[:, i, 0:tiles(r)] for i in range(10)]
                    nc.vector.reciprocal(s[7], s[6]).then_inc(own_dve, 1)
                    dve.wait_ge(own_dve, settled())
                    nc.vector.scalar_tensor_tensor(out=s[8], in0=s[0], scalar=-0.5, in1=s[7],
                                                   op0=ALU.mult, op1=ALU.mult)
                    nc.vector.tensor_tensor(s[3], o_sb[:, r % 2, 0:tiles(r), E], s[7], ALU.mult).then_inc(own_dve, 1)
                    dve.wait_ge(own_dve, settled())
                    nc.vector.scalar_tensor_tensor(out=s[4], in0=s[8], scalar=rsum[:, 0:1], in1=s[3],
                                                   op0=ALU.mult, op1=ALU.add).then_inc(own_dve, 1)
                    dve.wait_ge(own_dve, settled())
                    nc.vector.tensor_scalar(score[:, 0:tiles(r)], s[4], rsum[:, 1:2], None,
                                            ALU.add).then_inc(score_done, 1)
                elif kind == "rank" and k == 0:
                    dve.wait_ge(score_done, r + 1)
                    nc.vector.transpose(score_b[:, :], score[:, :]).then_inc(own_dve, 1)
                    dve.wait_ge(own_dve, settled())
                    other = score_b[:, None, :].to_broadcast([P, T, T])
                    this = score_b[:, :, None].to_broadcast([P, T, T])
                    nc.vector.tensor_tensor(gt[:, :, :], other, this, ALU.is_gt)
                    nc.vector.tensor_tensor(eq[:, :, :], other, this, ALU.is_equal).then_inc(own_dve, 1)
                    dve.wait_ge(own_dve, settled())
                elif kind == "rank":
                    dve.wait_ge(consts, 3)
                    nc.vector.tensor_tensor(eq[:, :, :], eq[:, :, :], before[:, :, :],
                                            ALU.mult).then_inc(own_dve, 1)
                    dve.wait_ge(own_dve, settled())
                    nc.vector.tensor_tensor(gt[:, :, :], gt[:, :, :], eq[:, :, :], ALU.add).then_inc(own_dve, 1)
                    dve.wait_ge(own_dve, settled())
                    nc.vector.tensor_reduce(rank_b[:, :], gt[:, :, :], AX_X, ALU.add).then_inc(own_dve, 1)
                    dve.wait_ge(own_dve, settled())
                    nc.vector.transpose(rank_n[:, :], rank_b[:, :]).then_inc(own_dve, 1)
                    dve.wait_ge(own_dve, settled())
                elif kind == "pick":
                    n = tiles(r)
                    if r:
                        last = ("gather", r - 1, 0)
                        dve.wait_ge(full(last), filled(last))
                    nc.vector.tensor_tensor(pick[:, 0:n, :], rank_of[:, None, :].to_broadcast([P, n, SEL]),
                                            rank_n[:, 0:n, None].to_broadcast([P, n, SEL]),
                                            ALU.is_equal).then_inc(pick_done, 1)
                    dve.wait_ge(sig_done, r + 1)
                    nc.vector.tensor_scalar(weight[:, r % 2, 0:n], small[:, 9, 0:n], 0.5, 0.5, ALU.mult,
                                            ALU.add).then_inc(own_dve, 1)
                    dve.wait_ge(own_dve, settled())
                    nc.vector.scalar_tensor_tensor(out=weight[:, r % 2, 0:n], in0=rank_n[:, 0:n], scalar=float(TOPK),
                                                   in1=weight[:, r % 2, 0:n], op0=ALU.is_lt,
                                                   op1=ALU.mult).then_inc(own_dve, 1)
                    dve.wait_ge(own_dve, settled())
                elif kind == "down":
                    dve.wait_ge(rest_in, REST)
                    nc.vector.tensor_tensor(
                        down[:, 0:tiles(r) // 2, :],
                        slot(step)[:, 0:tiles(r) // 2 * E].rearrange("p (n e) -> p n e", e=E),
                        b2_r[:, None, :].to_broadcast([P, tiles(r) // 2, E]), ALU.add).then_inc(read(step), 1)
                elif kind == "scatter":
                    dve.wait_ge(res_done, r + 1)
                    for n in range(tiles(r)):
                        res = x_nat[:, BEFORE[r] * QT + n, :]
                        src = slot(step)[:, n % 2 * BANK + n // 2 * E:][:, 0:E]
                        last = nc.vector.scalar_tensor_tensor(
                            out=res, in0=src, scalar=weight[:, r % 2, n:n + 1], in1=res, op0=ALU.mult,
                            op1=ALU.add)
                    last.then_inc(read(step), 1)

        @block.tensor
        def _(pe):
            for step in STEPS:
                kind, r, k = step
                if kind not in READERS:
                    continue
                for i in range(2 if kind == "state" else 1):
                    if reads_before(step, i):
                        pe.wait_ge(read(step, i), reads_before(step, i))
                dst = slot(step)
                banks = [slice(i * BANK, (i + 1) * BANK) for i in range(QUADS[r])]
                if kind == "turn_a":
                    pe.wait_ge(wa_in, 4 * 16)
                    pe.wait_ge(consts, 1)
                    for i, w in enumerate((wg_in[:, 0:E], wg_in[:, E:2 * E], wsoma_in[:, :])):
                        nc.tensor.transpose(dst[:, i * P:(i + 1) * P], w, ident[:, :])
                    nc.tensor.transpose(dst[:, 3 * P:3 * P + HN], wn1_in[:, :], ident[0:HN, 0:HN])
                    last = nc.tensor.transpose(dst[0:HN, BANK:BANK + P], wn2_in[:, :], ident[:, :])
                elif kind == "turn_b":
                    pe.wait_ge(wb_in, WB)
                    for i, w in enumerate((blend_in, wtemp_in, wout_in)):
                        last = nc.tensor.transpose(dst[:, i * P:(i + 1) * P], w[:, :], ident[:, :])
                elif kind == "turn_c":
                    pe.wait_ge(tabled, 2)
                    nc.tensor.transpose(dst[:, 0:P], sexp[:, :], ident[:, :])
                    last = nc.tensor.transpose(dst[:, P:2 * P], tail_row[:, :, :].rearrange("p b t -> p (b t)"),
                                               ident[:, :])
                elif kind == "turn_d":
                    pe.wait_ge(tabled, 2)
                    nc.tensor.matmul(dst[:, 0:2], wout_in[:, :], rw[:, :], start=True, stop=True)
                    last = nc.tensor.matmul(dst[:, 2:4], ones[:, :], rw[:, :], start=True, stop=True)
                elif kind == "xt":
                    pe.wait_ge(x_in[r], 16)
                    for n in range(tiles(r)):
                        last = nc.tensor.transpose(dst[:, n * P:(n + 1) * P], x_nat[:, BEFORE[r] * QT + n, :],
                                                   ident[:, :])
                elif kind in ("soma", "h1"):
                    pe.wait_ge(read(("turn_a", 0, 0)), reads_after(("turn_a", 0, 0)))
                    pe.wait_ge(read(("xt", r, 0)), reads_after(("xt", r, 0)))
                    w, rows = (wsoma_t, P) if kind == "soma" else (wn1_t, HN)
                    for half in banks:
                        last = nc.tensor.matmul(dst[0:rows, half], w, part(x_t, r, half.start, half.stop), start=True, stop=True)
                elif kind == "wg":
                    pe.wait_ge(ctx_done, r + 1)
                    for half in banks:
                        nc.tensor.matmul(dst[:, half], wgx_t, part(x_t, r, half.start, half.stop), start=True, stop=False)
                        last = nc.tensor.matmul(dst[:, half], wgc_t, part(ctx_acc, r, half.start, half.stop), start=False, stop=True)
                elif kind == "mod":
                    pe.wait_ge(read(("h1", r, 0)), reads_after(("h1", r, 0)))
                    for half in banks:
                        last = nc.tensor.matmul(dst[:, half], wn2_t[:, :], h1[:, r % 2, half], start=True, stop=True)
                elif kind == "nat":
                    pe.wait_ge(gated_done, r + 1)
                    pe.wait_ge(read(("mod", r, 0)), reads_after(("mod", r, 0)))
                    for i, src in enumerate((sig(r), gated(r))):
                        for n in range(QT):
                            tile = src[:, (k * QT + n) * P:(k * QT + n + 1) * P]
                            last = nc.tensor.transpose(dst[:, i * BANK + n * P:i * BANK + (n + 1) * P], tile,
                                                       ident[:, :])
                elif kind == "state":
                    q = BEFORE[r] + k
                    pe.wait_ge(read(("nat", r, k)), reads_after(("nat", r, k)))
                    for n in range(QT):
                        for b in range(BT):
                            rows = slice(b * T, b * T + L)
                            to = slot(step, b // 2)[:, b % 2 * BANK + n * E:][:, 0:E]
                            last = nc.tensor.matmul(to, mod_nat[rows, q % 2, n, :], gated_nat[rows, q % 2, n, :],
                                                    start=True, stop=True)
                            if n == QT - 1 and b % 2:
                                last.then_inc(full(step, b // 2), 1)
                    continue
                elif kind == "carry":
                    for i in range(2):
                        pe.wait_ge(read(("state", r, k), i), reads_after(("state", r, k), i))
                    for n in range(QT):
                        for b in range(BT):
                            i = n * BT + b
                            last = nc.tensor.matmul(dst[:, i * L:(i + 1) * L], state[:, b, n, :],
                                                    powers[:, 1:L + 1], start=True, stop=True)
                elif kind == "unit":
                    pe.wait_ge(split_done, r + 1)
                    pe.wait_ge(tabled, 3)
                    to = in_slot(dst, r, k)
                    parts = ((decayed_lo, mod_hi), (decayed_hi, mod_lo), (decayed_hi, mod_hi))
                    for i, (w, m) in enumerate(parts):
                        src = lagged(m[:, r % 2, 0:tiles(r) * P], r, k)
                        for h in range(QUADS[r]):
                            last = nc.tensor.matmul(to[:, h], w[:, k, :], src[:, h], start=(i == 0),
                                                    stop=(i == len(parts) - 1))
                elif kind == "gate":
                    pe.wait_ge(acc_done, (r + 1) * L)
                    for half in banks:
                        last = nc.tensor.matmul(dst[:, half], wtemp_t[:, :], part(ctx_acc, r, half.start, half.stop),
                                                start=True, stop=True)
                elif kind == "out":
                    pe.wait_ge(sg_done, r + 1)
                    for n in range(QT):
                        at = n // 2 * BANK + n % 2 * OW
                        tile = part(x_t, r, (k * QT + n) * P, (k * QT + n + 1) * P)
                        last = nc.tensor.matmul(dst[:, at:at + OW], tile, wout_t[:, :], start=True, stop=True)
                elif kind == "gather":
                    pe.wait_ge(pick_done, r + 1)
                    pe.wait_ge(norm_done, BEFORE[r + 1] * QT)
                    for n in range(tiles(r) // 2):
                        nc.tensor.transpose(dst[:, BANK + n * P:BANK + (n + 1) * P],
                                            pick[:, 2 * n:2 * n + 2, :].rearrange("p n k -> p (n k)"), ident[:, :])
                    for n in range(tiles(r)):
                        last = nc.tensor.matmul(dst[:, n * SEL:(n + 1) * SEL], o_sb[:, r % 2, n, 0:E], pick[:, n, :],
                                                start=True, stop=True)
                elif kind == "up":
                    pe.wait_ge(read(("gather", r, 0)), reads_after(("gather", r, 0)))
                    pe.wait_ge(rest_in, REST)
                    n_sel = tiles(r) * SEL
                    for i in range(2):
                        f = 2 * k + i
                        last = nc.tensor.matmul(dst[:, i * BANK:i * BANK + n_sel], w1_sb[:, f * P:(f + 1) * P],
                                                hid_t[:, 0:n_sel],
                                                start=True, stop=True)
                elif kind == "down":
                    for i in range(2):
                        pe.wait_ge(read(("up", r, i)), reads_after(("up", r, i)))
                    for n in range(tiles(r) // 2):
                        for f in range(NF):
                            at = f * tiles(r) * SEL + n * P
                            src = inner(r, at, at + P)
                            last = nc.tensor.matmul(dst[:, n * E:(n + 1) * E], src, w2_sb[:, f, :],
                                                    start=(f == 0), stop=(f == NF - 1))
                elif kind == "scatter":
                    pe.wait_ge(read(("down", r, 0)), reads_after(("down", r, 0)))
                    for n in range(tiles(r)):
                        rows = slice(n % 2 * SEL, (n % 2 + 1) * SEL)
                        last = nc.tensor.matmul(dst[:, n % 2 * BANK + n // 2 * E:][:, 0:E],
                                                pick_t[rows, n // 2, :], down[rows, n // 2, :],
                                                start=True, stop=True)
                last.then_inc(full(step), 1)


_INS = ["x", "condB_tauraws", "cond_256", "condB_bn2", "cond_1024", "L0_cond_tau_ctx", "L0_cond_Wg",
        "L0_cond_bg", "L0_cond_Wn1", "L0_cond_bn1", "L0_cond_Wsoma", "L0_cond_bsoma", "L0_cond_Wtemp",
        "L0_cond_btemp", "L0_cond_Wout", "L0_cond_gamma", "L0_cond_beta", "L0_ffn_w_router", "L0_ffn_W1",
        "L0_ffn_b1", "L0_ffn_W2", "L0_ffn_b2"]


def kernel(**inputs):
    import numpy as _np
    import concourse.bacc as _bacc
    from concourse import mybir as _mybir
    from concourse.bass_utils import run_bass_kernel_spmd as _run

    nc = _bacc.Bacc("TRN2", target_bir_lowering=False, num_devices=1)
    arrays, args = {}, []
    for name in _INS:
        a = _np.ascontiguousarray(inputs[name])
        if name == "L0_cond_tau_ctx":
            a = a.reshape(1, 1)
        arrays[f"in_{name}_dram"] = a
        args.append(nc.dram_tensor(f"in_{name}_dram", a.shape, _mybir.dt.from_np(a.dtype), kind="ExternalInput").ap())
    args.append(nc.dram_tensor("out_0_dram", (B, T, E), _mybir.dt.from_np(_np.dtype("float32")),
                               kind="ExternalOutput").ap())
    adaln_ffn(nc, *args)
    r = _run(nc, [arrays], core_ids=[0])
    return r.results[0]["out_0_dram"]
```

```python
from contextlib import ExitStack

import concourse.bass as bass
from concourse import mybir

P = 128
B, T, E, D, F, HN = 128, 32, 128, 128, 512, 32
TOPK = T // 2
L = T // 2
NCH = T // L
BT = P // T
QT = 4
BQ = BT * QT
QUADS = (1, 2, 2, 2, 1)
BEFORE = tuple(sum(QUADS[:r]) for r in range(len(QUADS) + 1))
R = len(QUADS)
assert BEFORE[R] * BQ == B
NQ = max(QUADS)
NT = NQ * QT
COLS = NT * P
BR = NQ * BQ
SEL = BT * TOPK
NSEL = NT * SEL
NS = NSEL // P
NF = F // P
BANK = 512
SLOT = 2 * BANK
NSLOT = 4
OW = E + 2
NP = 3

ALU = mybir.AluOpType
ACT = mybir.ActivationFunctionType
AX_X = mybir.AxisListType.X
F32 = mybir.dt.float32
F32R = mybir.dt.float32r
BF16 = mybir.dt.bfloat16

REST = 6 * 16
WB = 7 * 16


def tiles(r):
    return QUADS[r] * QT


ORDER = """
decay:0 turn_a:0 xt:0 context:0 xt:1 h1:0 h1:1 plus_beta:0 turn_b:0 plus_beta:1 context:1 mod:0 mod:1
wg:0 alpha:0 turn_c:0 xt:2 tables:0 split:0 gated:0 low:0 xt:3 wg:1 gated:1 h1:2 nat:0 plus_beta:2
state:0 plus_beta:3 unit:0.0 unit:0.1 nat:1 state:0.1 context:2 turn_d:0 h1:3 unit:0.8 split:1 unit:0.9
unit:0.2 unit:0.10 unit:0.15 xt:4 carry:0 unit:0.13 unit:0.3 unit:0.12 mod:2 unit:0.6 unit:0.5 low:1
unit:0.7 unit:0.11 carry:0.1 unit:0.14 unit:0.4 context:3 sum:0 unit:1.0 context:4 unit:1.10 unit:1.15
unit:1.1 unit:1.13 unit:1.9 nat:1.1 soma:0 gate:0 state:1 wg:2 split:2 soma_gate:0 state:1.1 out:0
stats:0 gated:2 carry:1 unit:1.4 carry:1.1 unit:1.3 state:1.2 wg:3 carry:1.2 plus_beta:4 var:0 std:0
unit:1.12 score:0 state:1.3 unit:1.2 mod:3 unit:1.7 unit:1.14 low:2 h1:4 rank:0 mod:4 unit:1.11 gated:3
normed:0 unit:1.5 tie:0 carry:1.3 nat:2 unit:1.8 wg:4 unit:1.6 sum:1 unit:2.0 pick:0 state:2 split:3
gather:0 soma:1 residual:0 carry:2 unit:2.11 gate:1 up:0 up:0.1 weight:0 soma_gate:1 unit:2.4 unit:2.15
unit:2.12 unit:2.8 unit:2.6 nat:2.1 state:2.1 state:2.2 down:0 out:1 low:3 out:1.1 unit:2.13 stats:1.1
stats:1 var:1 std:1 unit:2.14 unit:2.3 scatter:0 unit:2.7 unit:2.10 soma:2 score:1 rank:1 carry:2.1
nat:3 unit:2.2 tie:1 pick:1 state:2.3 carry:2.2 normed:1 unit:2.1 state:3 gather:1 carry:2.3 unit:2.9
up:1 unit:2.5 sum:2 up:1.1 unit:3.0 down:1 weight:1 gate:2 split:4 residual:1 gated:4 soma_gate:2
scatter:1 unit:3.12 soma:3 nat:3.1 state:3.1 out:2 stats:2 out:2.1 stats:2.1 var:2 unit:3.1 std:2
carry:3 score:2 nat:4 unit:3.15 unit:3.9 rank:2 carry:3.1 tie:2 normed:2 state:3.2 pick:2 unit:3.3
unit:3.7 unit:3.2 state:3.3 gather:2 unit:3.11 unit:3.5 unit:3.4 unit:3.8 carry:3.2 unit:3.6 up:2 low:4
unit:3.10 up:2.1 weight:2 unit:3.13 carry:3.3 unit:3.14 down:2 sum:3 unit:4.0 state:4 gate:3 residual:2
unit:4.7 unit:4.12 soma_gate:3 scatter:2 unit:4.9 carry:4 out:3 unit:4.13 unit:4.15 out:3.1 stats:3
unit:4.11 stats:3.1 unit:4.3 var:3 std:3 state:4.1 unit:4.14 score:3 unit:4.6 normed:3 rank:3 carry:4.1
soma:4 tie:3 pick:3 unit:4.1 unit:4.5 unit:4.2 gather:3 weight:3 unit:4.10 unit:4.4 unit:4.8 sum:4
residual:3 up:3 up:3.1 gate:4 soma_gate:4 out:4 stats:4 var:4 std:4 down:3 score:4 rank:4 tie:4 pick:4
scatter:3 normed:4 residual:4 gather:4 up:4 up:4.1 down:4 weight:4 scatter:4
"""


def parsed(word):
    kind, _, at = word.partition(":")
    r, _, k = at.partition(".")
    return kind, int(r), int(k or 0)


STEPS = [parsed(word) for word in ORDER.split()]

QUAD = [(r, k) for r in range(R) for k in range(QUADS[r])]

READERS = {"turn_a": 2, "turn_b": 2, "turn_c": 2, "turn_d": 2, "xt": 1, "soma": 1, "h1": 1, "wg": 1, "mod": 1,
           "nat": 2, "state": 1, "carry": 1, "unit": 1, "gate": 1, "out": 1, "gather": 2, "up": 2, "down": 1,
           "scatter": 1}
RING = [s for s in STEPS if s[0] in READERS]
USE = {s: n for n, s in enumerate(RING)}


def filled(step):
    return USE[step] // NSLOT + 1


def reads_before(step):
    n = USE[step]
    return sum(READERS[s[0]] for s in RING[n % NSLOT:n:NSLOT])


def reads_after(step):
    return reads_before(step) + READERS[step[0]]


assert max(STEPS.index(("context", r, 0)) for r in range(R)) < STEPS.index(("rank", 0, 0))


def adaln_ffn(nc, x, tau_raws, w_n2, b_n2, blend, tau_ctx, w_g, b_g, w_n1, b_n1, w_soma, b_soma,
              w_temp, b_temp, w_out, gamma, beta, w_router, w_1, b_1, w_2, b_2, out):
    with ExitStack() as ctx:
        def sb(name, shape, dt=F32):
            return ctx.enter_context(nc.sbuf_tensor(name, shape, dt))

        def sem(name):
            return ctx.enter_context(nc.semaphore(name))

        ring = ctx.enter_context(nc.psum_tensor("ring", [P, NSLOT, SLOT], F32))

        ident = sb("ident", [P, P])
        ones = sb("ones", [P, P])
        wg_in = sb("wg_in", [P, 2 * E])
        wn1_in = sb("wn1_in", [HN, E])
        wn2_in = sb("wn2_in", [P, HN])
        blend_in = sb("blend_in", [P, E])
        wsoma_in = sb("wsoma_in", [P, E])
        wtemp_in = sb("wtemp_in", [P, E])
        wout_in = sb("wout_in", [P, E])
        w1_sb = sb("w1_sb", [P, F])
        w2_sb = sb("w2_sb", [P, NF, E])
        turned_w = sb("turned_w", [P, 3 * P + HN])
        wgx_t, wgc_t, wsoma_t = (turned_w[:, i * P:(i + 1) * P] for i in range(3))
        wn1_t = turned_w[:, 3 * P:3 * P + HN]
        wn2_t = sb("wn2_t", [HN, D])
        wtemp_t = sb("wtemp_t", [P, E])
        wout_t = sb("wout_t", [P, OW])
        bg, bsoma, btemp = sb("bg", [P, 1]), sb("bsoma", [P, 1]), sb("btemp", [P, 1])
        bn1, bn2 = sb("bn1", [HN, 1]), sb("bn2", [P, 1])
        gamma_c, beta_c, router = sb("gamma_c", [P, 1]), sb("beta_c", [P, 1]), sb("router", [P, 1])
        b1_c = sb("b1_c", [P, NF])
        gamma_r, beta_r, b2_r = sb("gamma_r", [P, E]), sb("beta_r", [P, E]), sb("b2_r", [P, E])
        taus = sb("taus", [P, 2])
        tau_e, tau_s, alphas = sb("tau_e", [P, 2]), sb("tau_s", [P, 2]), sb("alphas", [P, 2])
        alpha, alpha_ctx = alphas[:, 0:1], alphas[:, 1:2]
        warm = sb("warm", [P, 1])
        smax, ssum, srec = sb("smax", [P, 1]), sb("ssum", [P, 1]), sb("srec", [P, 1])
        sexp = sb("sexp", [P, P])
        blend_t = sexp
        blend_w = sb("blend_w", [P, E])
        decayed_hi, decayed_lo = sb("decayed_hi", [P, L, E], F32R), sb("decayed_lo", [P, L, E], F32R)
        powers = sb("powers", [P, L + 1])
        tail_row = sb("tail_row", [P, BT, T])
        tail = sb("tail", [P, D])
        rw = sb("rw", [P, 2])
        rsum = sb("rsum", [P, 2])
        rank_of = sb("rank_of", [P, SEL])
        before = sb("before", [P, T, T], BF16)

        x_nat = sb("x_nat", [P, B // BT, E])
        x_t = sb("x_t", [P, B * T])
        ctx_acc = sb("ctx_acc", [P, B * T])
        gm = sb("gm", [P, 2 * B * T])
        soma = sb("soma", [P, 2, COLS])
        mod_hi, mod_lo = sb("mod_hi", [P, 2, COLS], F32R), sb("mod_lo", [P, 2, COLS], F32R)
        mod_nat = sb("mod_nat", [P, 2, QT, D])
        gated_nat = sb("gated_nat", [P, 2, QT, E])
        state = sb("state", [P, BT, QT, E])
        carried = sb("carried", [P, 2, BR, L])
        prod = sb("prod", [P, NP, SLOT])
        prod_res = sb("prod_res", [P, NT, E])
        o_sb = sb("o_sb", [P, 2, NT, OW])
        stats = sb("stats", [P, NT, 6])
        small = sb("small", [P, 10, NT])
        score = sb("score", [P, T])
        score_b = sb("score_b", [P, T])
        compared = sb("compared", [P, 2, T, T], BF16)
        gt, eq = compared[:, 0], compared[:, 1]
        ctx_decay = compared[:, :, :, :].rearrange("p i t u -> p (i t u)").bitcast(F32)
        rank_b = sb("rank_b", [P, T])
        rank_n = sb("rank_n", [P, T])
        weight = sb("weight", [P, 2, NT])
        pick = sb("pick", [P, NT, SEL])
        pick_t = sb("pick_t", [P, NS, P])
        hid_t = sb("hid_t", [P, NSEL])
        down = sb("down", [P, NS, E])
        h1 = sb("h1", [HN, 2, COLS])
        decayed = state[:, :, :, :].rearrange("p b n e -> p (b n) e")

        x_in = [sem(f"x_in{r}") for r in range(R)]
        wa_in, ba_in, tau_in, wb_in, rest_in = (sem(n) for n in ("wa_in", "ba_in", "tau_in", "wb_in", "rest_in"))
        own_pool, own_dve = sem("own_pool"), sem("own_dve")
        consts = sem("consts")
        alphas_done = sem("alphas_done")
        exped = sem("exped")
        tabled = sem("tabled")
        slot_full = [sem(f"slot_full{i}") for i in range(NSLOT)]
        slot_read = [sem(f"slot_read{i}") for i in range(NSLOT)]
        ctx_done = sem("ctx_done")
        gated_done, split_done = sem("gated_done"), sem("split_done")
        hi_done = sem("hi_done")
        acc_done = sem("acc_done")
        sg_done = sem("sg_done")
        var_done, std_done = sem("var_done"), sem("std_done")
        norm_done = sem("norm_done")
        score_done, sig_done = sem("score_done"), sem("sig_done")
        pick_done = sem("pick_done")
        res_done, xb_done = sem("res_done"), sem("xb_done")
        y_out = sem("y_out")

        x_dram = x.rearrange("b t e -> (b t) e").rearrange("(n p) e -> p n e", p=P)
        y_dram = out.rearrange("b t e -> (b t) e").rearrange("(n p) e -> p n e", p=P)

        def col(v):
            return v.rearrange("(p o) -> p o", o=1)

        def row(v):
            return v.rearrange("(o n) -> o n", o=1).to_broadcast([P, v.shape[0]])

        def slot(step):
            return ring[:, USE[step] % NSLOT, :]

        def cols_of(step):
            return slot(step)[:, 0:tiles(step[1]) * P]

        def full(step):
            return slot_full[USE[step] % NSLOT]

        def read(step):
            return slot_read[USE[step] % NSLOT]

        def tiles_of(buf, r):
            return buf[:, BEFORE[r] * QT:BEFORE[r + 1] * QT]

        def part(buf, r, first=0, last=None):
            last = tiles(r) * P if last is None else last
            return buf[:, BEFORE[r] * BANK + first:BEFORE[r] * BANK + last]

        def gated(r):
            return gm[:, 2 * BEFORE[r] * BANK:][:, 0:QUADS[r] * BANK]

        def sig(r):
            return gm[:, (2 * BEFORE[r] + QUADS[r]) * BANK:][:, 0:QUADS[r] * BANK]

        def inner(r, first, last):
            return gm[:, 2 * BEFORE[r] * BANK + first:2 * BEFORE[r] * BANK + last]

        def lagged(buf, r, lag, shift=0):
            t0 = shift * lag
            return buf.rearrange("p (h b t) -> p h t b", h=QUADS[r], t=L)[:, :, t0:t0 + L - lag, :]

        def in_slot(buf, r, lag):
            n = (L - lag) * NCH * BQ
            return buf[:, 0:QUADS[r] * BANK].rearrange("p (h n) -> p h n", h=QUADS[r])[:, :, 0:n].rearrange(
                "p h (t b) -> p h t b", t=L - lag)


        LAGS = [[k for kind, p, k in STEPS if kind == "unit" and p == r] for r in range(R)]
        assert all(lags[0] == 0 for lags in LAGS)

        def sums_to(r, i):
            return r * L + i

        block = ctx.enter_context(nc.Block())

        @block.sync
        def _(sp):
            sp.dma_start(tiles_of(x_nat, 0), tiles_of(x_dram, 0)).then_inc(x_in[0], 16)
            sp.dma_start(wn1_in[:, :], w_n1).then_inc(wa_in, 16)
            sp.dma_start(wn2_in[:, :], w_n2).then_inc(wa_in, 16)
            sp.dma_start(taus[:, 1:2], tau_ctx.to_broadcast([P, 1])).then_inc(tau_in, 16)
            sp.dma_start(tiles_of(x_nat, 1), tiles_of(x_dram, 1)).then_inc(x_in[1], 16)
            sp.dma_start(bg[:, :], col(b_g)).then_inc(ba_in, 16)
            sp.dma_start(bn2[:, :], col(b_n2)).then_inc(ba_in, 16)
            for dst, src in ((blend_in[:, :], blend), (wtemp_in[:, :], w_temp), (wout_in[:, :], w_out),
                             (btemp[:, :], col(b_temp)), (gamma_c[:, :], col(gamma)), (beta_c[:, :], col(beta)),
                             (router[:, :], col(w_router))):
                sp.dma_start(dst, src).then_inc(wb_in, 16)
            sp.dma_start(tiles_of(x_nat, 2), tiles_of(x_dram, 2)).then_inc(x_in[2], 16)
            sp.dma_start(tiles_of(x_nat, 3), tiles_of(x_dram, 3)).then_inc(x_in[3], 16)
            sp.dma_start(tiles_of(x_nat, 4), tiles_of(x_dram, 4)).then_inc(x_in[4], 16)
            sp.dma_start(w1_sb[:, :], w_1).then_inc(rest_in, 16)
            sp.dma_start(w2_sb[:, :, :], w_2.rearrange("(k p) e -> p k e", p=P)).then_inc(rest_in, 16)
            sp.dma_start(b1_c[:, :], b_1.rearrange("(k p) -> p k", p=P),
                         allow_slow_non_contiguous=True).then_inc(rest_in, 16)
            sp.dma_start(gamma_r[:, :], row(gamma)).then_inc(rest_in, 16)
            sp.dma_start(beta_r[:, :], row(beta)).then_inc(rest_in, 16)
            sp.dma_start(b2_r[:, :], row(b_2)).then_inc(rest_in, 16)
            for r in range(R):
                step = ("scatter", r, 0)
                sp.wait_ge(read(step), reads_after(step))
                sp.dma_start(tiles_of(y_dram, r), tiles_of(x_nat, r)).then_inc(y_out, 16)
            sp.wait_ge(y_out, R * 16)

        @block.gpsimd
        def _(pool):
            nc.gpsimd.memset(ident[:, :], 0.0).then_inc(own_pool, 1)
            nc.gpsimd.memset(ones[:, :], 1.0).then_inc(own_pool, 1)
            pool.wait_ge(own_pool, 2)
            nc.gpsimd.affine_select(out=ident[:, :], in_=ident[:, :], compare_op=ALU.not_equal, fill=1.0,
                                    base=0, pattern=[[-1, P]], channel_multiplier=1).then_inc(consts, 1)
            nc.gpsimd.memset(before[:, :, :], 1.0).then_inc(own_pool, 1)
            nc.gpsimd.iota(rank_of[:, :], pattern=[[0, BT], [1, TOPK]], base=0, channel_multiplier=0,
                           allow_small_or_imprecise_dtypes=True).then_inc(own_pool, 1)
            pool.wait_ge(own_pool, 4)
            places = rank_of[:, :].rearrange("p (b j) -> p b j", b=BT)
            nc.gpsimd.affine_select(out=places, in_=places, compare_op=ALU.is_ge, fill=-1.0, base=0,
                                    pattern=[[-T, BT], [0, TOPK]], channel_multiplier=1).then_inc(own_pool, 1)
            pool.wait_ge(own_pool, 5)
            nc.gpsimd.affine_select(out=places, in_=places, compare_op=ALU.is_ge, fill=-1.0, base=T - 1,
                                    pattern=[[T, BT], [0, TOPK]], channel_multiplier=-1).then_inc(consts, 1)
            nc.gpsimd.affine_select(out=before[:, :, :], in_=before[:, :, :], compare_op=ALU.is_ge, fill=0.0,
                                    base=-1, pattern=[[1, T], [-1, T]], channel_multiplier=0).then_inc(consts, 1)
            pool.wait_ge(rest_in, REST)
            for step in STEPS:
                kind, r, k = step
                if kind == "plus_beta":
                    turned = ("xt", r, 0)
                    pool.wait_ge(full(turned), filled(turned))
                    x_r = tiles_of(x_nat, r)
                    nc.gpsimd.tensor_tensor(x_r, x_r, beta_r[:, None, :].to_broadcast([P, tiles(r), E]),
                                            ALU.add).then_inc(xb_done, 1)
                elif kind == "unit" and k > 0:
                    i = LAGS[r].index(k)
                    n = r * (L - 1) + i - 1
                    dst = lagged(part(ctx_acc, r), r, k, shift=1)
                    pool.wait_ge(read(step), reads_after(step))
                    if i > 1:
                        pool.wait_ge(acc_done, sums_to(r, i - 1))
                    nc.gpsimd.tensor_tensor(dst, dst, in_slot(prod[:, n % NP, :], r, k), ALU.add).then_inc(acc_done, 1)
                elif kind == "sum":
                    for h in range(2 * QUADS[r]):
                        pool.wait_ge(read(("carry", r, h)), reads_after(("carry", r, h)))
                    pool.wait_ge(acc_done, sums_to(r, L - 1))
                    dst = part(ctx_acc, r).rearrange("p (b t) -> p b t", t=T)[:, :, L:]
                    nc.gpsimd.tensor_tensor(dst, dst, carried[:, r % 2, 0:QUADS[r] * BQ], ALU.add).then_inc(acc_done, 1)
                elif kind == "residual":
                    pool.wait_ge(norm_done, BEFORE[r + 1] * QT)
                    if r:
                        pool.wait_ge(res_done, r)
                    nc.gpsimd.tensor_tensor(prod_res[:, 0:tiles(r), :], o_sb[:, r % 2, 0:tiles(r), 0:E],
                                            gamma_r[:, None, :].to_broadcast([P, tiles(r), E]),
                                            ALU.mult).then_inc(own_pool, 1)
                    pool.wait_ge(own_pool, 6 + r)
                    pool.wait_ge(xb_done, r + 1)
                    nc.gpsimd.tensor_tensor(tiles_of(x_nat, r), tiles_of(x_nat, r), prod_res[:, 0:tiles(r), :],
                                            ALU.add).then_inc(res_done, 1)

        @block.scalar
        def _(act):
            act.dma_start(wg_in[:, :], w_g).then_inc(wa_in, 16)
            act.dma_start(taus[:, 0:1], col(tau_raws)).then_inc(tau_in, 16)
            act.dma_start(wsoma_in[:, :], w_soma).then_inc(wa_in, 16)
            act.dma_start(bsoma[:, :], col(b_soma)).then_inc(ba_in, 16)
            act.dma_start(bn1[:, :], col(b_n1)).then_inc(ba_in, 16)
            for step in STEPS:
                kind, r, k = step
                if kind in ("xt", "soma", "h1", "wg", "mod", "nat", "carry", "gate", "out", "gather", "up"):
                    act.wait_ge(full(step), filled(step))
                if kind == "decay":
                    act.wait_ge(tau_in, 2 * 16)
                    nc.scalar.activation(tau_e[:, :], taus[:, :], ACT.Exp).then_inc(exped, 1)
                    act.wait_ge(ba_in, 4 * 16)
                elif kind == "turn_b":
                    act.wait_ge(alphas_done, 2)
                    nc.scalar.activation(sexp[:, :], blend_t[:, :], ACT.Exp, bias=smax[:, :],
                                         accum_out=ssum[:, :]).then_inc(exped, 1)
                elif kind == "turn_d":
                    act.wait_ge(wb_in, WB)
                elif kind == "xt":
                    nc.scalar.activation(part(x_t, r), cols_of(step), ACT.Copy).then_inc(read(step), 1)
                elif kind == "soma":
                    if r >= 2:
                        act.wait_ge(sg_done, r - 1)
                    nc.scalar.activation(soma[:, r % 2, 0:tiles(r) * P], cols_of(step), ACT.Gelu,
                                         bias=bsoma[:, :]).then_inc(read(step), 1)
                elif kind == "h1":
                    if r >= 2:
                        last = ("mod", r - 2, 0)
                        act.wait_ge(full(last), filled(last))
                    nc.scalar.activation(h1[:, r % 2, 0:tiles(r) * P], cols_of(step)[0:HN], ACT.Gelu,
                                         bias=bn1[:, :]).then_inc(read(step), 1)
                elif kind == "wg":
                    nc.scalar.activation(gated(r), cols_of(step), ACT.Sigmoid, bias=bg[:, :]).then_inc(read(step), 1)
                elif kind == "mod":
                    nc.scalar.activation(sig(r), cols_of(step), ACT.Sigmoid, bias=bn2[:, :]).then_inc(read(step), 1)
                elif kind == "split":
                    act.wait_ge(read(("mod", r, 0)), reads_after(("mod", r, 0)))
                    if r >= 2:
                        last = ("unit", r - 2, LAGS[r - 2][-1])
                        act.wait_ge(full(last), filled(last))
                    nc.scalar.activation(mod_hi[:, r % 2, 0:tiles(r) * P], sig(r), ACT.Copy,
                                         bias=0.5).then_inc(hi_done, 1)
                elif kind == "nat":
                    q = BEFORE[r] + k
                    if q >= 2:
                        last = ("state", QUAD[q - 2][0], 2 * QUAD[q - 2][1] + 1)
                        act.wait_ge(full(last), filled(last))
                    nc.scalar.activation(gated_nat[:, q % 2, :, :].rearrange("p n e -> p (n e)"),
                                         slot(step)[:, BANK:], ACT.Copy).then_inc(read(step), 1)
                elif kind == "carry":
                    if r >= 2 and k == 0:
                        act.wait_ge(acc_done, sums_to(r - 1, 0))
                    q, pair = k // 2, k % 2 * 2
                    dst = carried[:, r % 2, q * BQ:(q + 1) * BQ, :].rearrange("p (n b) t -> p n b t", b=BT)
                    src = slot(step)[:, 0:BQ // 2 * L].rearrange("p (n b t) -> p n b t", n=QT, b=2)
                    nc.scalar.activation(dst[:, :, pair:pair + 2], src, ACT.Copy).then_inc(read(step), 1)
                elif kind == "gate":
                    last = ("soma", r, 0)
                    act.wait_ge(full(last), filled(last))
                    nc.scalar.activation(part(x_t, r), cols_of(step), ACT.Sigmoid,
                                         bias=btemp[:, :]).then_inc(read(step), 1)
                elif kind == "out":
                    if r >= 2 and k == 0:
                        last = ("gather", r - 2, 0)
                        act.wait_ge(res_done, r - 1)
                        act.wait_ge(full(last), filled(last))
                    src = slot(step).rearrange("p (h n) -> p h n", h=2)[:, :, 0:2 * OW]
                    dst = o_sb[:, r % 2, k * QT:(k + 1) * QT, :].rearrange("p (h n) w -> p h (n w)", h=2)
                    nc.scalar.activation(dst, src, ACT.Copy).then_inc(read(step), 1)
                elif kind == "std":
                    nc.scalar.activation(warm[:, :], ones[:, 0:1], ACT.Sqrt)
                    act.wait_ge(var_done, r + 1)
                    nc.scalar.activation(small[:, 6, 0:tiles(r)], small[:, 5, 0:tiles(r)], ACT.Sqrt).then_inc(std_done, 1)
                elif kind == "normed":
                    act.wait_ge(score_done, r + 1)
                    for n in range(tiles(r)):
                        nc.scalar.activation(o_sb[:, r % 2, n, 0:E], o_sb[:, r % 2, n, 0:E], ACT.Identity,
                                             bias=small[:, 8, n:n + 1],
                                             scale=small[:, 7, n:n + 1]).then_inc(norm_done, 1)
                    nc.scalar.activation(small[:, 9, 0:tiles(r)], score[:, 0:tiles(r)], ACT.Tanh,
                                         scale=0.5).then_inc(sig_done, 1)
                elif kind == "gather":
                    nc.scalar.activation(hid_t[:, 0:tiles(r) * SEL], slot(step)[:, 0:tiles(r) * SEL], ACT.Identity, bias=beta_c[:, :],
                                         scale=gamma_c[:, :]).then_inc(read(step), 1)
                    nc.scalar.activation(pick_t[:, 0:tiles(r) // 2, :].rearrange("p n k -> p (n k)"),
                                         slot(step)[:, BANK:BANK + tiles(r) // 2 * P],
                                         ACT.Copy).then_inc(read(step), 1)
                elif kind == "up":
                    if r == 0 and k == 0:
                        act.wait_ge(rest_in, REST)
                    n_sel = tiles(r) * SEL
                    for i in range(2):
                        f = 2 * k + i
                        nc.scalar.activation(inner(r, f * n_sel, (f + 1) * n_sel),
                                             slot(step)[:, i * BANK:i * BANK + n_sel], ACT.Gelu_apprx_tanh,
                                             bias=b1_c[:, f:f + 1]).then_inc(read(step), 1)

        @block.vector
        def _(dve):
            own = [0]

            def settled():
                own[0] += 1
                return own[0]

            nc.vector.memset(powers[:, 0:1], 1.0)
            nc.vector.memset(score[:, :], 0.0)
            nc.vector.memset(tail_row[:, :, :], 1.0).then_inc(own_dve, 1)
            dve.wait_ge(own_dve, settled())
            for step in STEPS:
                kind, r, k = step
                if kind in ("turn_a", "turn_b", "turn_c", "turn_d", "nat", "state", "unit", "down", "scatter"):
                    dve.wait_ge(full(step), filled(step))
                if kind == "turn_a":
                    nc.vector.tensor_copy(turned_w[:, :], slot(step)[:, 0:3 * P + HN]).then_inc(read(step), 1)
                    nc.vector.tensor_copy(wn2_t[:, :], slot(step)[0:HN, BANK:BANK + P]).then_inc(read(step), 1)
                elif kind == "decay":
                    dve.wait_ge(exped, 1)
                    nc.vector.tensor_scalar(tau_s[:, :], tau_e[:, :], 1.0, None, ALU.add).then_inc(own_dve, 1)
                    dve.wait_ge(own_dve, settled())
                    nc.vector.reciprocal(alphas[:, :], tau_s[:, :]).then_inc(own_dve, 1)
                    dve.wait_ge(own_dve, settled())
                    nc.vector.tensor_copy(ctx_decay, alpha_ctx.to_broadcast([P, COLS])).then_inc(own_dve, 1)
                    dve.wait_ge(own_dve, settled())
                    nc.vector.memset(ctx_decay.rearrange("p (b t) -> p b t", t=T)[:, :, 0:1],
                                     0.0).then_inc(alphas_done, 1)
                elif kind == "turn_b":
                    nc.vector.tensor_copy(blend_t[:, :], slot(step)[:, 0:P]).then_inc(own_dve, 1)
                    dve.wait_ge(own_dve, settled())
                    nc.vector.tensor_reduce(smax[:, :], blend_t[:, :], AX_X, ALU.max,
                                            negate=True).then_inc(alphas_done, 1)
                    nc.vector.tensor_copy(wtemp_t[:, :], slot(step)[:, P:2 * P]).then_inc(read(step), 1)
                    nc.vector.tensor_copy(wout_t[:, 0:E], slot(step)[:, 2 * P:3 * P]).then_inc(read(step), 1)
                elif kind == "alpha":
                    dve.wait_ge(alphas_done, 1)
                    dve.wait_ge(consts, 1)
                    nc.vector.tensor_tensor_scan(powers[:, 1:L + 1], alpha.to_broadcast([P, L]), ones[:, 0:L], 1.0,
                                                 ALU.mult, ALU.mult).then_inc(own_dve, 1)
                    dve.wait_ge(own_dve, settled())
                    for t in range(L):
                        nc.vector.tensor_copy(tail_row[:, :, t:t + 1],
                                              powers[:, None, L - 1 - t:L - t].to_broadcast([P, BT, 1]))
                    dve.wait_ge(exped, 2)
                    nc.vector.reciprocal(srec[:, :], ssum[:, :]).then_inc(own_dve, 1)
                    dve.wait_ge(own_dve, settled())
                    nc.vector.tensor_scalar(sexp[:, :], sexp[:, :], srec[:, :], None, ALU.mult).then_inc(tabled, 1)
                    dve.wait_ge(wb_in, WB)
                    nc.vector.tensor_tensor(rw[:, 0:1], gamma_c[:, :], router[:, :], ALU.mult)
                    nc.vector.tensor_tensor(rw[:, 1:2], beta_c[:, :], router[:, :], ALU.mult).then_inc(tabled, 1)
                elif kind == "turn_c":
                    nc.vector.tensor_copy(blend_w[:, :], slot(step)[:, 0:P]).then_inc(read(step), 1)
                    nc.vector.tensor_copy(tail[:, :], slot(step)[:, P:2 * P]).then_inc(read(step), 1)
                elif kind == "tables":
                    turned = ("turn_c", 0, 0)
                    dve.wait_ge(read(turned), reads_after(turned))
                    nc.vector.tensor_tensor(decayed, blend_w[:, None, :].to_broadcast([P, L, E]),
                                            powers[:, 0:L, None].to_broadcast([P, L, E]),
                                            ALU.mult).then_inc(own_dve, 1)
                    dve.wait_ge(own_dve, settled())
                    nc.vector.tensor_copy(decayed_hi[:, :, :], decayed).then_inc(own_dve, 1)
                    dve.wait_ge(own_dve, settled())
                    nc.vector.tensor_tensor(decayed_lo[:, :, :], decayed, decayed_hi[:, :, :].bitcast(F32),
                                            ALU.subtract).then_inc(tabled, 1)
                elif kind == "turn_d":
                    nc.vector.tensor_copy(wout_t[:, E:E + 2], slot(step)[:, 0:2]).then_inc(read(step), 1)
                    nc.vector.tensor_copy(rsum[:, :], slot(step)[:, 2:4]).then_inc(read(step), 1)
                elif kind == "context":
                    dve.wait_ge(alphas_done, 1)
                    dve.wait_ge(read(("xt", r, 0)), reads_after(("xt", r, 0)))
                    nc.vector.tensor_tensor_scan(part(ctx_acc, r), ctx_decay[:, 0:tiles(r) * P], part(x_t, r), 0.0, ALU.mult,
                                                 ALU.add).then_inc(ctx_done, 1)
                elif kind == "gated":
                    dve.wait_ge(read(("wg", r, 0)), reads_after(("wg", r, 0)))
                    nc.vector.tensor_tensor(gated(r), gated(r), part(x_t, r),
                                            ALU.mult).then_inc(gated_done, 1)
                elif kind == "low":
                    dve.wait_ge(read(("mod", r, 0)), reads_after(("mod", r, 0)))
                    if r >= 2:
                        last = ("unit", r - 2, LAGS[r - 2][-1])
                        dve.wait_ge(full(last), filled(last))
                    dve.wait_ge(hi_done, r + 1)
                    nc.vector.scalar_tensor_tensor(
                        out=mod_lo[:, r % 2, 0:tiles(r) * P], in0=sig(r), scalar=0.5,
                        in1=mod_hi[:, r % 2, 0:tiles(r) * P].bitcast(F32), op0=ALU.add, op1=ALU.subtract).then_inc(split_done, 1)
                elif kind == "nat":
                    q = BEFORE[r] + k
                    if q >= 2:
                        last = ("state", QUAD[q - 2][0], 2 * QUAD[q - 2][1] + 1)
                        dve.wait_ge(full(last), filled(last))
                    nc.vector.scalar_tensor_tensor(
                        out=mod_nat[:, q % 2], in0=slot(step)[:, 0:BANK].rearrange("p (n d) -> p n d", n=QT),
                        scalar=0.5, in1=tail[:, None, :].to_broadcast([P, QT, D]), op0=ALU.add,
                        op1=ALU.mult).then_inc(read(step), 1)
                elif kind == "state":
                    q, pair = BEFORE[r] + k // 2, k % 2 * 2
                    if q:
                        last = ("carry", QUAD[q - 1][0], 2 * QUAD[q - 1][1] + k % 2)
                        dve.wait_ge(full(last), filled(last))
                    nc.vector.tensor_tensor(
                        state[:, pair:pair + 2].rearrange("p b n e -> p (b n) e"),
                        slot(step).rearrange("p (n e) -> p n e", e=E),
                        blend_w[:, None, :].to_broadcast([P, 2 * QT, E]), ALU.mult).then_inc(read(step), 1)
                elif kind == "unit":
                    dve.wait_ge(gated_done, r + 1)
                    if k:
                        n = r * (L - 1) + LAGS[r].index(k) - 1
                        if n >= NP:
                            m = n - NP
                            dve.wait_ge(acc_done, sums_to(m // (L - 1), m % (L - 1) + 1))
                        dst = in_slot(prod[:, n % NP, :], r, k)
                    else:
                        dst = lagged(part(ctx_acc, r), r, 0)
                    nc.vector.tensor_tensor(dst, in_slot(slot(step), r, k), lagged(gated(r), r, k),
                                            ALU.mult).then_inc(read(step), 1)
                elif kind == "soma_gate":
                    for last in (("soma", r, 0), ("gate", r, 0)):
                        dve.wait_ge(read(last), reads_after(last))
                    nc.vector.tensor_tensor(part(x_t, r), part(x_t, r), soma[:, r % 2, 0:tiles(r) * P],
                                            ALU.mult).then_inc(sg_done, 1)
                elif kind == "stats":
                    dve.wait_ge(read(("out", r, k)), reads_after(("out", r, k)))
                    for n in range(k * QT, (k + 1) * QT):
                        last = nc.vector.bn_stats(stats[:, n, :], o_sb[:, r % 2, n, 0:E])
                    last.then_inc(own_dve, 1)
                    dve.wait_ge(own_dve, settled())
                elif kind == "var":
                    s = [small[:, i, 0:tiles(r)] for i in range(10)]
                    m_e, v_e, m_o, v_o = (stats[:, 0:tiles(r), i] for i in (1, 2, 4, 5))
                    nc.vector.tensor_tensor(s[0], m_e, m_o, ALU.add)
                    nc.vector.tensor_tensor(s[3], v_e, v_o, ALU.add)
                    nc.vector.tensor_tensor(s[1], m_e, m_o, ALU.subtract).then_inc(own_dve, 1)
                    dve.wait_ge(own_dve, settled())
                    nc.vector.tensor_tensor(s[2], s[1], s[1], ALU.mult).then_inc(own_dve, 1)
                    dve.wait_ge(own_dve, settled())
                    nc.vector.scalar_tensor_tensor(out=s[4], in0=s[2], scalar=E / 4.0, in1=s[3],
                                                   op0=ALU.mult, op1=ALU.add).then_inc(own_dve, 1)
                    dve.wait_ge(own_dve, settled())
                    nc.vector.tensor_scalar(s[5], s[4], 1.0 / E, 1e-5, ALU.mult, ALU.add).then_inc(var_done, 1)
                elif kind == "score":
                    dve.wait_ge(std_done, r + 1)
                    s = [small[:, i, 0:tiles(r)] for i in range(10)]
                    nc.vector.reciprocal(s[7], s[6]).then_inc(own_dve, 1)
                    dve.wait_ge(own_dve, settled())
                    nc.vector.scalar_tensor_tensor(out=s[8], in0=s[0], scalar=-0.5, in1=s[7],
                                                   op0=ALU.mult, op1=ALU.mult)
                    nc.vector.tensor_tensor(s[3], o_sb[:, r % 2, 0:tiles(r), E], s[7], ALU.mult).then_inc(own_dve, 1)
                    dve.wait_ge(own_dve, settled())
                    nc.vector.scalar_tensor_tensor(out=s[4], in0=s[8], scalar=rsum[:, 0:1], in1=s[3],
                                                   op0=ALU.mult, op1=ALU.add).then_inc(own_dve, 1)
                    dve.wait_ge(own_dve, settled())
                    nc.vector.tensor_scalar(score[:, 0:tiles(r)], s[4], rsum[:, 1:2], None,
                                            ALU.add).then_inc(score_done, 1)
                elif kind == "rank":
                    dve.wait_ge(score_done, r + 1)
                    nc.vector.transpose(score_b[:, :], score[:, :]).then_inc(own_dve, 1)
                    dve.wait_ge(own_dve, settled())
                    other = score_b[:, None, :].to_broadcast([P, T, T])
                    this = score_b[:, :, None].to_broadcast([P, T, T])
                    nc.vector.tensor_tensor(gt[:, :, :], other, this, ALU.is_gt)
                    nc.vector.tensor_tensor(eq[:, :, :], other, this, ALU.is_equal).then_inc(own_dve, 1)
                    dve.wait_ge(own_dve, settled())
                elif kind == "tie":
                    dve.wait_ge(consts, 3)
                    nc.vector.tensor_tensor(eq[:, :, :], eq[:, :, :], before[:, :, :],
                                            ALU.mult).then_inc(own_dve, 1)
                    dve.wait_ge(own_dve, settled())
                    nc.vector.tensor_tensor(gt[:, :, :], gt[:, :, :], eq[:, :, :], ALU.add).then_inc(own_dve, 1)
                    dve.wait_ge(own_dve, settled())
                    nc.vector.tensor_reduce(rank_b[:, :], gt[:, :, :], AX_X, ALU.add).then_inc(own_dve, 1)
                    dve.wait_ge(own_dve, settled())
                    nc.vector.transpose(rank_n[:, :], rank_b[:, :]).then_inc(own_dve, 1)
                    dve.wait_ge(own_dve, settled())
                elif kind == "pick":
                    n = tiles(r)
                    if r:
                        last = ("gather", r - 1, 0)
                        dve.wait_ge(full(last), filled(last))
                    nc.vector.tensor_tensor(pick[:, 0:n, :], rank_of[:, None, :].to_broadcast([P, n, SEL]),
                                            rank_n[:, 0:n, None].to_broadcast([P, n, SEL]),
                                            ALU.is_equal).then_inc(pick_done, 1)
                elif kind == "weight":
                    n = tiles(r)
                    dve.wait_ge(sig_done, r + 1)
                    nc.vector.tensor_scalar(weight[:, r % 2, 0:n], small[:, 9, 0:n], 0.5, 0.5, ALU.mult,
                                            ALU.add).then_inc(own_dve, 1)
                    dve.wait_ge(own_dve, settled())
                    nc.vector.scalar_tensor_tensor(out=weight[:, r % 2, 0:n], in0=rank_n[:, 0:n], scalar=float(TOPK),
                                                   in1=weight[:, r % 2, 0:n], op0=ALU.is_lt,
                                                   op1=ALU.mult).then_inc(own_dve, 1)
                    dve.wait_ge(own_dve, settled())
                elif kind == "down":
                    dve.wait_ge(rest_in, REST)
                    nc.vector.tensor_tensor(
                        down[:, 0:tiles(r) // 2, :],
                        slot(step)[:, 0:tiles(r) // 2 * E].rearrange("p (n e) -> p n e", e=E),
                        b2_r[:, None, :].to_broadcast([P, tiles(r) // 2, E]), ALU.add).then_inc(read(step), 1)
                elif kind == "scatter":
                    dve.wait_ge(res_done, r + 1)
                    for n in range(tiles(r)):
                        res = x_nat[:, BEFORE[r] * QT + n, :]
                        src = slot(step)[:, n % 2 * BANK + n // 2 * E:][:, 0:E]
                        last = nc.vector.scalar_tensor_tensor(
                            out=res, in0=src, scalar=weight[:, r % 2, n:n + 1], in1=res, op0=ALU.mult,
                            op1=ALU.add)
                    last.then_inc(read(step), 1)

        @block.tensor
        def _(pe):
            for step in STEPS:
                kind, r, k = step
                if kind not in READERS:
                    continue
                if reads_before(step):
                    pe.wait_ge(read(step), reads_before(step))
                dst = slot(step)
                banks = [slice(i * BANK, (i + 1) * BANK) for i in range(QUADS[r])]
                if kind == "turn_a":
                    pe.wait_ge(wa_in, 4 * 16)
                    pe.wait_ge(consts, 1)
                    for i, w in enumerate((wg_in[:, 0:E], wg_in[:, E:2 * E], wsoma_in[:, :])):
                        nc.tensor.transpose(dst[:, i * P:(i + 1) * P], w, ident[:, :])
                    nc.tensor.transpose(dst[:, 3 * P:3 * P + HN], wn1_in[:, :], ident[0:HN, 0:HN])
                    last = nc.tensor.transpose(dst[0:HN, BANK:BANK + P], wn2_in[:, :], ident[:, :])
                elif kind == "turn_b":
                    pe.wait_ge(wb_in, WB)
                    for i, w in enumerate((blend_in, wtemp_in, wout_in)):
                        last = nc.tensor.transpose(dst[:, i * P:(i + 1) * P], w[:, :], ident[:, :])
                elif kind == "turn_c":
                    pe.wait_ge(tabled, 2)
                    nc.tensor.transpose(dst[:, 0:P], sexp[:, :], ident[:, :])
                    last = nc.tensor.transpose(dst[:, P:2 * P], tail_row[:, :, :].rearrange("p b t -> p (b t)"),
                                               ident[:, :])
                elif kind == "turn_d":
                    pe.wait_ge(tabled, 2)
                    nc.tensor.matmul(dst[:, 0:2], wout_in[:, :], rw[:, :], start=True, stop=True)
                    last = nc.tensor.matmul(dst[:, 2:4], ones[:, :], rw[:, :], start=True, stop=True)
                elif kind == "xt":
                    pe.wait_ge(x_in[r], 16)
                    pe.wait_ge(consts, 1)
                    for n in range(tiles(r)):
                        last = nc.tensor.transpose(dst[:, n * P:(n + 1) * P], x_nat[:, BEFORE[r] * QT + n, :],
                                                   ident[:, :])
                elif kind in ("soma", "h1"):
                    pe.wait_ge(read(("turn_a", 0, 0)), reads_after(("turn_a", 0, 0)))
                    pe.wait_ge(read(("xt", r, 0)), reads_after(("xt", r, 0)))
                    w, rows = (wsoma_t, P) if kind == "soma" else (wn1_t, HN)
                    for half in banks:
                        last = nc.tensor.matmul(dst[0:rows, half], w, part(x_t, r, half.start, half.stop), start=True, stop=True)
                elif kind == "wg":
                    pe.wait_ge(ctx_done, r + 1)
                    for half in banks:
                        nc.tensor.matmul(dst[:, half], wgx_t, part(x_t, r, half.start, half.stop), start=True, stop=False)
                        last = nc.tensor.matmul(dst[:, half], wgc_t, part(ctx_acc, r, half.start, half.stop), start=False, stop=True)
                elif kind == "mod":
                    pe.wait_ge(read(("h1", r, 0)), reads_after(("h1", r, 0)))
                    for half in banks:
                        last = nc.tensor.matmul(dst[:, half], wn2_t[:, :], h1[:, r % 2, half], start=True, stop=True)
                elif kind == "nat":
                    pe.wait_ge(gated_done, r + 1)
                    pe.wait_ge(read(("mod", r, 0)), reads_after(("mod", r, 0)))
                    for i, src in enumerate((sig(r), gated(r))):
                        for n in range(QT):
                            tile = src[:, (k * QT + n) * P:(k * QT + n + 1) * P]
                            last = nc.tensor.transpose(dst[:, i * BANK + n * P:i * BANK + (n + 1) * P], tile,
                                                       ident[:, :])
                elif kind == "state":
                    q, pair = BEFORE[r] + k // 2, k % 2 * 2
                    nat = ("nat", r, k // 2)
                    pe.wait_ge(read(nat), reads_after(nat))
                    for n in range(QT):
                        for b in range(2):
                            rows = slice((pair + b) * T, (pair + b) * T + L)
                            last = nc.tensor.matmul(dst[:, b * BANK + n * E:][:, 0:E], mod_nat[rows, q % 2, n, :],
                                                    gated_nat[rows, q % 2, n, :], start=True, stop=True)
                elif kind == "carry":
                    pair = k % 2 * 2
                    made = ("state", r, k)
                    pe.wait_ge(read(made), reads_after(made))
                    for n in range(QT):
                        for b in range(2):
                            i = 2 * n + b
                            last = nc.tensor.matmul(dst[:, i * L:(i + 1) * L], state[:, pair + b, n, :],
                                                    powers[:, 1:L + 1], start=True, stop=True)
                elif kind == "unit":
                    pe.wait_ge(split_done, r + 1)
                    pe.wait_ge(tabled, 3)
                    to = in_slot(dst, r, k)
                    parts = ((decayed_lo, mod_hi), (decayed_hi, mod_lo), (decayed_hi, mod_hi))
                    for i, (w, m) in enumerate(parts):
                        src = lagged(m[:, r % 2, 0:tiles(r) * P], r, k)
                        for h in range(QUADS[r]):
                            last = nc.tensor.matmul(to[:, h], w[:, k, :], src[:, h], start=(i == 0),
                                                    stop=(i == len(parts) - 1))
                elif kind == "gate":
                    pe.wait_ge(acc_done, (r + 1) * L)
                    for half in banks:
                        last = nc.tensor.matmul(dst[:, half], wtemp_t[:, :], part(ctx_acc, r, half.start, half.stop),
                                                start=True, stop=True)
                elif kind == "out":
                    pe.wait_ge(sg_done, r + 1)
                    for n in range(QT):
                        at = n // 2 * BANK + n % 2 * OW
                        tile = part(x_t, r, (k * QT + n) * P, (k * QT + n + 1) * P)
                        last = nc.tensor.matmul(dst[:, at:at + OW], tile, wout_t[:, :], start=True, stop=True)
                elif kind == "gather":
                    pe.wait_ge(pick_done, r + 1)
                    pe.wait_ge(norm_done, BEFORE[r + 1] * QT)
                    for n in range(tiles(r) // 2):
                        nc.tensor.transpose(dst[:, BANK + n * P:BANK + (n + 1) * P],
                                            pick[:, 2 * n:2 * n + 2, :].rearrange("p n k -> p (n k)"), ident[:, :])
                    for n in range(tiles(r)):
                        last = nc.tensor.matmul(dst[:, n * SEL:(n + 1) * SEL], o_sb[:, r % 2, n, 0:E], pick[:, n, :],
                                                start=True, stop=True)
                elif kind == "up":
                    pe.wait_ge(read(("gather", r, 0)), reads_after(("gather", r, 0)))
                    pe.wait_ge(rest_in, REST)
                    n_sel = tiles(r) * SEL
                    for i in range(2):
                        f = 2 * k + i
                        last = nc.tensor.matmul(dst[:, i * BANK:i * BANK + n_sel], w1_sb[:, f * P:(f + 1) * P],
                                                hid_t[:, 0:n_sel],
                                                start=True, stop=True)
                elif kind == "down":
                    for i in range(2):
                        pe.wait_ge(read(("up", r, i)), reads_after(("up", r, i)))
                    for n in range(tiles(r) // 2):
                        for f in range(NF):
                            at = f * tiles(r) * SEL + n * P
                            src = inner(r, at, at + P)
                            last = nc.tensor.matmul(dst[:, n * E:(n + 1) * E], src, w2_sb[:, f, :],
                                                    start=(f == 0), stop=(f == NF - 1))
                elif kind == "scatter":
                    pe.wait_ge(read(("down", r, 0)), reads_after(("down", r, 0)))
                    for n in range(tiles(r)):
                        rows = slice(n % 2 * SEL, (n % 2 + 1) * SEL)
                        last = nc.tensor.matmul(dst[:, n % 2 * BANK + n // 2 * E:][:, 0:E],
                                                pick_t[rows, n // 2, :], down[rows, n // 2, :],
                                                start=True, stop=True)
                last.then_inc(full(step), 1)


_INS = ["x", "condB_tauraws", "cond_256", "condB_bn2", "cond_1024", "L0_cond_tau_ctx", "L0_cond_Wg",
        "L0_cond_bg", "L0_cond_Wn1", "L0_cond_bn1", "L0_cond_Wsoma", "L0_cond_bsoma", "L0_cond_Wtemp",
        "L0_cond_btemp", "L0_cond_Wout", "L0_cond_gamma", "L0_cond_beta", "L0_ffn_w_router", "L0_ffn_W1",
        "L0_ffn_b1", "L0_ffn_W2", "L0_ffn_b2"]


def kernel(**inputs):
    import numpy as _np
    import concourse.bacc as _bacc
    from concourse import mybir as _mybir
    from concourse.bass_utils import run_bass_kernel_spmd as _run

    nc = _bacc.Bacc("TRN2", target_bir_lowering=False, num_devices=1)
    arrays, args = {}, []
    for name in _INS:
        a = _np.ascontiguousarray(inputs[name])
        if name == "L0_cond_tau_ctx":
            a = a.reshape(1, 1)
        arrays[f"in_{name}_dram"] = a
        args.append(nc.dram_tensor(f"in_{name}_dram", a.shape, _mybir.dt.from_np(a.dtype), kind="ExternalInput").ap())
    args.append(nc.dram_tensor("out_0_dram", (B, T, E), _mybir.dt.from_np(_np.dtype("float32")),
                               kind="ExternalOutput").ap())
    adaln_ffn(nc, *args)
    r = _run(nc, [arrays], core_ids=[0])
    return r.results[0]["out_0_dram"]
```
